# Optimizing a Trainium2 kernel written in Bass

```python
import numpy as np
import jax
import jax.numpy as jnp

def _softmax(x, axis=-1):
    return jax.nn.softmax(x, axis=axis)

def _gelu(x):
    return jax.nn.gelu(x, approximate=True)

def _silu(x):
    return jax.nn.silu(x)

def _sigmoid(x):
    return jax.nn.sigmoid(x)

def _layernorm(x, axis=-1, eps=1e-05):
    m = jnp.mean(x, axis=axis, keepdims=True)
    v = jnp.var(x, axis=axis, keepdims=True)
    return (x - m) / jnp.sqrt(v + eps)

def _scatter_add(tgt, idx, src, axis=0):
    return tgt.at[idx].add(src)

def _segment_sum(src, seg, n):
    return jax.ops.segment_sum(src, seg, n)
kernel_name = 'mk_gnn_preln_d4_gnn_r8_56a604'

def setup_inputs(seed: int=0):
    np.random.seed(seed)
    _w = jnp.asarray

    def _rec_inputs():
        import jax
        import jax.numpy as jnp
        _gk = jax.random.key(seed)
        x = -0.001003 + 1 * jax.random.normal(jax.random.fold_in(_gk, 1), (384, 512), jnp.float32)
        _s = jax.random.randint(jax.random.fold_in(_gk, 2), (6144,), 0, 384, jnp.int32)
        _d = jax.random.randint(jax.random.fold_in(_gk, 3), (6144,), 0, 384, jnp.int32)
        _loop = jnp.arange(384, dtype=jnp.int32)
        src = jnp.concatenate([_s, _d, _loop])
        dst = jnp.concatenate([_d, _s, _loop])
        _o = jnp.argsort(dst, stable=True)
        src = src[_o]
        dst = dst[_o]
        edge_attr_128 = 0.000283511 + 1.00007 * jax.random.normal(jax.random.fold_in(_gk, 11), (12672, 128), jnp.float32)
        edge_type_2 = jax.random.randint(jax.random.fold_in(_gk, 13), (12672,), 0, 2, jnp.int32)
        return (x, src, dst, edge_attr_128, edge_type_2)
    x, src, dst, edge_attr_128, edge_type_2 = _rec_inputs()

    def _L0_gnn_setup():
        import jax, jax.numpy as jnp
        import numpy as np
        H = 8
        D = 64
        N = 384
        IN_DIM = 512
        E = 12288
        key = jax.random.key(seed)
        ks = jax.random.split(key, 8)
        x = jax.random.normal(ks[0], (N, IN_DIM), dtype=jnp.float32)
        edge_index = jax.random.randint(ks[1], (2, E), 0, N, dtype=jnp.int64)
        s = 1.0 / np.sqrt(IN_DIM)
        Wq = jax.random.normal(ks[2], (IN_DIM, H * D), dtype=jnp.float32) * s
        Wk = jax.random.normal(ks[3], (IN_DIM, H * D), dtype=jnp.float32) * s
        Wv = jax.random.normal(ks[4], (IN_DIM, H * D), dtype=jnp.float32) * s
        bq = jax.random.normal(ks[5], (H * D,), dtype=jnp.float32) * 0.01
        bk = jax.random.normal(ks[6], (H * D,), dtype=jnp.float32) * 0.01
        bv = jax.random.normal(ks[7], (H * D,), dtype=jnp.float32) * 0.01
        return {'x': x, 'edge_index': edge_index, 'Wq': Wq, 'Wk': Wk, 'Wv': Wv, 'bq': bq, 'bk': bk, 'bv': bv}
    _L0_gnn_all = _L0_gnn_setup()
    _L0_gnn_in = {k: v for k, v in _L0_gnn_all.items() if k in ('Wq', 'Wk', 'Wv', 'bq', 'bk', 'bv')}
    del _L0_gnn_all

    def _L1_gnn_setup():
        import jax, jax.numpy as jnp
        import numpy as np
        NUM_RELATIONS = 2
        NUM_BASES = 30
        HIDDEN = 512
        N_NODES = 1250
        N_EDGES = 20000

        def rgcn_gate_layer(x, row, col, edge_type, basis, att, gate_w, root, bias):
            H = x.shape[1]
            w = jnp.einsum('rb,bio->rio', att, basis)
            x_j = x[col]
            msgs = []
            for r in range(NUM_RELATIONS):
                gate = jax.nn.sigmoid(x_j @ gate_w[r, :, 0])
                msgs.append(gate[:, None] * x_j @ w[r])
            msg = jnp.where((edge_type == 0)[:, None], msgs[0], msgs[1])
            agg = jax.ops.segment_sum(msg, row, num_segments=x.shape[0])
            return agg + x @ root + bias
        key = jax.random.key(seed)
        ks = jax.random.split(key, 16)
        H, R, B = (HIDDEN, NUM_RELATIONS, NUM_BASES)
        bound = 1.0 / np.sqrt(B * H)
        u = lambda k, shape: jax.random.uniform(k, shape, jnp.float32, -bound, bound)
        inp = {'x': jax.random.normal(ks[0], (N_NODES, H), jnp.float32), 'edge_index': jax.random.randint(ks[1], (2, N_EDGES), 0, N_NODES, jnp.int32), 'edge_type': jax.random.randint(ks[2], (N_EDGES,), 0, R, jnp.int32), 'basis1': u(ks[3], (B, H, H)), 'att1': u(ks[4], (R, B)), 'gate_w1': u(ks[5], (R, H, 1)), 'root1': u(ks[6], (H, H)), 'bias1': u(ks[7], (H,)), 'basis2': u(ks[8], (B, H, H)), 'att2': u(ks[9], (R, B)), 'gate_w2': u(ks[10], (R, H, 1)), 'root2': u(ks[11], (H, H)), 'bias2': u(ks[12], (H,))}
        return inp
    _L1_gnn_all = _L1_gnn_setup()
    _L1_gnn_in = {k: v for k, v in _L1_gnn_all.items() if k in ('basis1', 'att1', 'gate_w1', 'root1', 'bias1', 'basis2', 'att2', 'gate_w2', 'root2', 'bias2')}
    del _L1_gnn_all

    def _L2_gnn_setup():
        import jax, jax.numpy as jnp
        import numpy as np
        NEG_SLOPE = 0.2
        HEADS = 8

        def gat_conv(x, src, dst, W, att_src, att_dst, bias, heads, out_ch):
            N = x.shape[0]
            h = (x @ W).reshape(N, heads, out_ch)
            a_src = jnp.einsum('nhc,hc->nh', h, att_src)
            a_dst = jnp.einsum('nhc,hc->nh', h, att_dst)
            e = jax.nn.leaky_relu(a_src[src] + a_dst[dst], NEG_SLOPE)
            m = jax.ops.segment_max(e, dst, num_segments=N)
            m = jnp.where(jnp.isfinite(m), m, jnp.zeros_like(m))
            ex = jnp.exp(e - m[dst])
            s = jax.ops.segment_sum(ex, dst, num_segments=N)
            alpha = ex / (s[dst] + 1e-16)
            msg = h[src] * alpha[:, :, None]
            out = jax.ops.segment_sum(msg, dst, num_segments=N)
            return out.reshape(N, heads * out_ch) + bias
        key = jax.random.key(seed)
        ks = jax.random.split(key, 12)
        N, F_in, nhid, heads, ncls, E = (2500, 512, 128, HEADS, 64, 25000)
        x = jax.random.normal(ks[0], (N, F_in), dtype=jnp.float32)
        edge_index = jax.random.randint(ks[1], (2, E), 0, N, dtype=jnp.int32)

        def lin(k, fi, fo):
            return jax.random.normal(k, (fi, fo), dtype=jnp.float32) / np.sqrt(fi)
        W1 = lin(ks[2], F_in, heads * nhid)
        att_src1 = jax.random.normal(ks[3], (heads, nhid), dtype=jnp.float32) / np.sqrt(nhid)
        att_dst1 = jax.random.normal(ks[4], (heads, nhid), dtype=jnp.float32) / np.sqrt(nhid)
        b1 = jnp.zeros((heads * nhid,), dtype=jnp.float32)
        W2 = lin(ks[5], heads * nhid, heads * ncls)
        att_src2 = jax.random.normal(ks[6], (heads, ncls), dtype=jnp.float32) / np.sqrt(ncls)
        att_dst2 = jax.random.normal(ks[7], (heads, ncls), dtype=jnp.float32) / np.sqrt(ncls)
        b2 = jnp.zeros((heads * ncls,), dtype=jnp.float32)
        return {'x': x, 'edge_index': edge_index, 'W1': W1, 'att_src1': att_src1, 'att_dst1': att_dst1, 'b1': b1, 'W2': W2, 'att_src2': att_src2, 'att_dst2': att_dst2, 'b2': b2}
    _L2_gnn_all = _L2_gnn_setup()
    _L2_gnn_in = {k: v for k, v in _L2_gnn_all.items() if k in ('W1', 'att_src1', 'att_dst1', 'b1', 'W2', 'att_src2', 'att_dst2', 'b2')}
    del _L2_gnn_all

    def _L3_gnn_setup():
        import jax, jax.numpy as jnp
        import numpy as np
        N, E = (1250, 18750)
        HD, ED = (512, 128)
        BN_EPS = 1e-05
        key = jax.random.key(seed)
        ks = jax.random.split(key, 16)
        s = 0.02
        return {'h': jax.random.normal(ks[0], (N, HD), jnp.float32), 'edge_index': jax.random.randint(ks[1], (2, E), 0, N, jnp.int32), 'edge_attr': jax.random.normal(ks[2], (E, ED), jnp.float32), 'W1': jax.random.normal(ks[3], (HD, HD + ED), jnp.float32) * s, 'b1': jnp.zeros((HD,), jnp.float32), 'W2': jax.random.normal(ks[4], (HD, HD), jnp.float32) * s, 'b2': jnp.zeros((HD,), jnp.float32), 'W_ih': jax.random.normal(ks[5], (3 * HD, HD), jnp.float32) * s, 'W_hh': jax.random.normal(ks[6], (3 * HD, HD), jnp.float32) * s, 'b_ih': jnp.zeros((3 * HD,), jnp.float32), 'b_hh': jnp.zeros((3 * HD,), jnp.float32), 'gamma': jnp.ones((HD,), jnp.float32), 'beta': jnp.zeros((HD,), jnp.float32), 'run_mean': jnp.zeros((HD,), jnp.float32), 'run_var': jnp.ones((HD,), jnp.float32)}
    _L3_gnn_all = _L3_gnn_setup()
    _L3_gnn_in = {k: v for k, v in _L3_gnn_all.items() if k in ('W1', 'b1', 'W2', 'b2', 'W_ih', 'W_hh', 'b_ih', 'b_hh', 'gamma', 'beta', 'run_mean', 'run_var')}
    del _L3_gnn_all
    return {'x': x, 'src': src, 'dst': dst, 'edge_attr_128': edge_attr_128, 'edge_type_2': edge_type_2, 'L0_gnn_Wq': _L0_gnn_in['Wq'], 'L0_gnn_Wk': _L0_gnn_in['Wk'], 'L0_gnn_Wv': _L0_gnn_in['Wv'], 'L0_gnn_bq': _L0_gnn_in['bq'], 'L0_gnn_bk': _L0_gnn_in['bk'], 'L0_gnn_bv': _L0_gnn_in['bv'], 'L1_gnn_basis1': _L1_gnn_in['basis1'], 'L1_gnn_att1': _L1_gnn_in['att1'], 'L1_gnn_gate_w1': _L1_gnn_in['gate_w1'], 'L1_gnn_root1': _L1_gnn_in['root1'], 'L1_gnn_bias1': _L1_gnn_in['bias1'], 'L1_gnn_basis2': _L1_gnn_in['basis2'], 'L1_gnn_att2': _L1_gnn_in['att2'], 'L1_gnn_gate_w2': _L1_gnn_in['gate_w2'], 'L1_gnn_root2': _L1_gnn_in['root2'], 'L1_gnn_bias2': _L1_gnn_in['bias2'], 'L2_gnn_W1': _L2_gnn_in['W1'], 'L2_gnn_att_src1': _L2_gnn_in['att_src1'], 'L2_gnn_att_dst1': _L2_gnn_in['att_dst1'], 'L2_gnn_b1': _L2_gnn_in['b1'], 'L2_gnn_W2': _L2_gnn_in['W2'], 'L2_gnn_att_src2': _L2_gnn_in['att_src2'], 'L2_gnn_att_dst2': _L2_gnn_in['att_dst2'], 'L2_gnn_b2': _L2_gnn_in['b2'], 'L3_gnn_W1': _L3_gnn_in['W1'], 'L3_gnn_b1': _L3_gnn_in['b1'], 'L3_gnn_W2': _L3_gnn_in['W2'], 'L3_gnn_b2': _L3_gnn_in['b2'], 'L3_gnn_W_ih': _L3_gnn_in['W_ih'], 'L3_gnn_W_hh': _L3_gnn_in['W_hh'], 'L3_gnn_b_ih': _L3_gnn_in['b_ih'], 'L3_gnn_b_hh': _L3_gnn_in['b_hh'], 'L3_gnn_gamma': _L3_gnn_in['gamma'], 'L3_gnn_beta': _L3_gnn_in['beta'], 'L3_gnn_run_mean': _L3_gnn_in['run_mean'], 'L3_gnn_run_var': _L3_gnn_in['run_var']}

def reference(x, src, dst, edge_attr_128, edge_type_2, L0_gnn_Wq, L0_gnn_Wk, L0_gnn_Wv, L0_gnn_bq, L0_gnn_bk, L0_gnn_bv, L1_gnn_basis1, L1_gnn_att1, L1_gnn_gate_w1, L1_gnn_root1, L1_gnn_bias1, L1_gnn_basis2, L1_gnn_att2, L1_gnn_gate_w2, L1_gnn_root2, L1_gnn_bias2, L2_gnn_W1, L2_gnn_att_src1, L2_gnn_att_dst1, L2_gnn_b1, L2_gnn_W2, L2_gnn_att_src2, L2_gnn_att_dst2, L2_gnn_b2, L3_gnn_W1, L3_gnn_b1, L3_gnn_W2, L3_gnn_b2, L3_gnn_W_ih, L3_gnn_W_hh, L3_gnn_b_ih, L3_gnn_b_hh, L3_gnn_gamma, L3_gnn_beta, L3_gnn_run_mean, L3_gnn_run_var):
    import jax
    import jax.numpy as jnp

    def _L0_gnn_ref(x, edge_index, Wq, Wk, Wv, bq, bk, bv):
        import jax, jax.numpy as jnp
        import numpy as np
        H = 8
        D = 64
        N = 384
        IN_DIM = 512
        E = 12288

        def proj(W, b):
            return (x @ W + b).reshape(N, H, D).transpose(1, 0, 2)
        q, k, v = (proj(Wq, bq), proj(Wk, bk), proj(Wv, bv))
        scores = jnp.einsum('hnd,hmd->hnm', q, k) / jnp.sqrt(jnp.float32(D))
        src, dst = (edge_index[0], edge_index[1])
        masked = jnp.zeros_like(scores).at[-1, src, dst].set(scores[-1, src, dst])
        att = jax.nn.softmax(masked, axis=-1)
        out = jnp.einsum('hnm,hmd->hnd', att, v)
        return out.transpose(1, 0, 2).reshape(N, H * D)

    def _L1_gnn_ref(x, edge_index, edge_type, basis1, att1, gate_w1, root1, bias1, basis2, att2, gate_w2, root2, bias2):
        import jax, jax.numpy as jnp
        import numpy as np
        NUM_RELATIONS = 2
        NUM_BASES = 30
        HIDDEN = 512
        N_NODES = 1250
        N_EDGES = 20000

        def rgcn_gate_layer(x, row, col, edge_type, basis, att, gate_w, root, bias):
            H = x.shape[1]
            w = jnp.einsum('rb,bio->rio', att, basis)
            x_j = x[col]
            msgs = []
            for r in range(NUM_RELATIONS):
                gate = jax.nn.sigmoid(x_j @ gate_w[r, :, 0])
                msgs.append(gate[:, None] * x_j @ w[r])
            msg = jnp.where((edge_type == 0)[:, None], msgs[0], msgs[1])
            agg = jax.ops.segment_sum(msg, row, num_segments=x.shape[0])
            return agg + x @ root + bias
        row, col = (edge_index[0], edge_index[1])
        h = jax.nn.relu(rgcn_gate_layer(x, row, col, edge_type, basis1, att1, gate_w1, root1, bias1))
        out = rgcn_gate_layer(h, row, col, edge_type, basis2, att2, gate_w2, root2, bias2)
        return out

    def _L2_gnn_ref(x, edge_index, W1, att_src1, att_dst1, b1, W2, att_src2, att_dst2, b2):
        import jax, jax.numpy as jnp
        import numpy as np
        NEG_SLOPE = 0.2
        HEADS = 8

        def gat_conv(x, src, dst, W, att_src, att_dst, bias, heads, out_ch):
            N = x.shape[0]
            h = (x @ W).reshape(N, heads, out_ch)
            a_src = jnp.einsum('nhc,hc->nh', h, att_src)
            a_dst = jnp.einsum('nhc,hc->nh', h, att_dst)
            e = jax.nn.leaky_relu(a_src[src] + a_dst[dst], NEG_SLOPE)
            m = jax.ops.segment_max(e, dst, num_segments=N)
            m = jnp.where(jnp.isfinite(m), m, jnp.zeros_like(m))
            ex = jnp.exp(e - m[dst])
            s = jax.ops.segment_sum(ex, dst, num_segments=N)
            alpha = ex / (s[dst] + 1e-16)
            msg = h[src] * alpha[:, :, None]
            out = jax.ops.segment_sum(msg, dst, num_segments=N)
            return out.reshape(N, heads * out_ch) + bias
        N = x.shape[0]
        nhid = att_src1.shape[1]
        ncls = att_src2.shape[1]
        loop = jnp.arange(N, dtype=edge_index.dtype)
        src = jnp.concatenate([edge_index[0], loop])
        dst = jnp.concatenate([edge_index[1], loop])
        h = gat_conv(x, src, dst, W1, att_src1, att_dst1, b1, HEADS, nhid)
        h = jax.nn.relu(h)
        out = gat_conv(h, src, dst, W2, att_src2, att_dst2, b2, HEADS, ncls)
        return jax.nn.log_softmax(out, axis=1)

    def _L3_gnn_ref(h, edge_index, edge_attr, W1, b1, W2, b2, W_ih, W_hh, b_ih, b_hh, gamma, beta, run_mean, run_var):
        import jax, jax.numpy as jnp
        import numpy as np
        N, E = (1250, 18750)
        HD, ED = (512, 128)
        BN_EPS = 1e-05
        src, dst = (edge_index[0], edge_index[1])
        m_in = jnp.concatenate([h[src], edge_attr], axis=1)
        m = jax.nn.relu(m_in @ W1.T + b1) @ W2.T + b2
        agg = jax.ops.segment_sum(m, dst, num_segments=h.shape[0])
        gi = agg @ W_ih.T + b_ih
        gh = h @ W_hh.T + b_hh
        i_r, i_z, i_n = jnp.split(gi, 3, axis=1)
        h_r, h_z, h_n = jnp.split(gh, 3, axis=1)
        r = jax.nn.sigmoid(i_r + h_r)
        z = jax.nn.sigmoid(i_z + h_z)
        n = jnp.tanh(i_n + r * h_n)
        h_new = (1.0 - z) * n + z * h
        bn = gamma * (h_new - run_mean) * jax.lax.rsqrt(run_var + BN_EPS) + beta
        return h + bn
    edge_index = jnp.stack([src, dst])
    h = jnp.maximum(_layernorm(x, axis=-1), 0.0)
    x = x + _L0_gnn_ref(h, edge_index, L0_gnn_Wq, L0_gnn_Wk, L0_gnn_Wv, L0_gnn_bq, L0_gnn_bk, L0_gnn_bv)
    h = jnp.maximum(_layernorm(x, axis=-1), 0.0)
    x = x + _L1_gnn_ref(h, edge_index, edge_type_2, L1_gnn_basis1, L1_gnn_att1, L1_gnn_gate_w1, L1_gnn_root1, L1_gnn_bias1, L1_gnn_basis2, L1_gnn_att2, L1_gnn_gate_w2, L1_gnn_root2, L1_gnn_bias2)
    h = jnp.maximum(_layernorm(x, axis=-1), 0.0)
    x = x + _L2_gnn_ref(h, edge_index, L2_gnn_W1, L2_gnn_att_src1, L2_gnn_att_dst1, L2_gnn_b1, L2_gnn_W2, L2_gnn_att_src2, L2_gnn_att_dst2, L2_gnn_b2)
    h = jnp.maximum(_layernorm(x, axis=-1), 0.0)
    x = x + _L3_gnn_ref(h, edge_index, edge_attr_128, L3_gnn_W1, L3_gnn_b1, L3_gnn_W2, L3_gnn_b2, L3_gnn_W_ih, L3_gnn_W_hh, L3_gnn_b_ih, L3_gnn_b_hh, L3_gnn_gamma, L3_gnn_beta, L3_gnn_run_mean, L3_gnn_run_var)
    return x

_drawn_inputs = setup_inputs


def setup_inputs(seed=0):
    import zlib

    import numpy as np

    out = dict(_drawn_inputs(seed))
    spreads = {'L2_gnn_b1': (0.0, 0.408),
     'L2_gnn_b2': (0.0, 0.272),
     'L3_gnn_b1': (0.0, 0.363),
     'L3_gnn_b2': (0.0, 0.1),
     'L3_gnn_b_ih': (0.0, 0.8),
     'L3_gnn_b_hh': (0.0, 0.8),
     'L3_gnn_gamma': (1.0, 0.6),
     'L3_gnn_beta': (0.0, 0.473),
     'L3_gnn_run_mean': (0.0, 0.435),
     'L3_gnn_run_var': (1.0, 0.6)}
    factors = {'edge_attr_128': 5.464,
     'L0_gnn_Wq': 8.0,
     'L0_gnn_Wk': 8.0,
     'L0_gnn_bq': 64.0,
     'L0_gnn_bk': 64.0,
     'L0_gnn_bv': 8.0,
     'L1_gnn_basis1': 8.0,
     'L1_gnn_att1': 8.0,
     'L1_gnn_gate_w1': 8.0,
     'L1_gnn_root1': 8.0,
     'L1_gnn_bias1': 31.602,
     'L1_gnn_basis2': 8.0,
     'L1_gnn_att2': 8.0,
     'L1_gnn_gate_w2': 8.0,
     'L1_gnn_root2': 8.0,
     'L1_gnn_bias2': 63.698,
     'L2_gnn_att_src1': 55.276,
     'L2_gnn_att_dst1': 64.0,
     'L2_gnn_att_src2': 64.0,
     'L2_gnn_att_dst2': 64.0,
     'L3_gnn_W_hh': 4.063}
    for name, (base, spread) in spreads.items():
        noise = np.random.default_rng([zlib.crc32(name.encode()), seed]).standard_normal(out[name].shape)
        drawn = base * np.exp(spread * noise) if base else spread * noise
        out[name] = jnp.asarray(drawn.astype(out[name].dtype))
    for name, factor in factors.items():
        out[name] = (out[name] * factor).astype(out[name].dtype)
    return out
```

```python
from contextlib import ExitStack

import concourse.bass as bass
import concourse.mybir as mybir
from concourse.alu_op_type import AluOpType as ALU

ACT = mybir.ActivationFunctionType
AX_X = mybir.AxisListType.X
F32 = mybir.dt.float32
F32R = mybir.dt.float32r
BF16 = mybir.dt.bfloat16
F16 = mybir.dt.float16
I32 = mybir.dt.int32

P = 128
N = 384
NT = N // P
F = 512
FC = F // P
E = 12672
ET = E // P
ED = 128
HEADS = 8
D0 = F // HEADS
BASES = 30
REL = 2
LN_EPS = 1e-5
BN_EPS = 1e-5
SLOPE = 0.2
FAR = -1e30

C1, C2 = 128, 64
MIX_V = 18
MIX_G = BASES - MIX_V
HALF = FC * F // 2
UV = 2 * MIX_V
UG = 2 * MIX_G
EB = 3
CB = 18
CT = -(-ET // CB)
LB = 9
LC = 3


def build(nc, a, out):
    with ExitStack() as ctx:
        def sb(name, shape, dt=F32):
            return ctx.enter_context(nc.sbuf_tensor(name, shape, dt))

        def sem(name):
            return ctx.enter_context(nc.semaphore(name))

        ps = ctx.enter_context(nc.psum_tensor("ps", [P, 8, 512], F32))

        mixm = sb("mixm", [P, 26624])
        ring_v = mixm[:, 0:4096].rearrange("p (k n) -> p k n", k=4)
        ring_g = mixm[:, 4096:6144].rearrange("p (k n) -> p k n", k=2)
        prod = mixm[:, 6144:10240].rearrange("p (k r n) -> p k r n", k=2, r=REL)
        acc_g = [mixm[:, o:o + 4096] for o in (10240, 18432)]
        w_mix = [mixm[:, o:o + 4096] for o in (14336, 22528)]

        def quarter(t, r, h):
            return t[:, (2 * r + h) * HALF:(2 * r + h + 1) * HALF]

        node = sb("node", [P, 10752])
        roots = node[:, 0:4096].rearrange("p (l c n) -> p l c n", l=2, c=FC)
        wv = node[:, 4096:6144].rearrange("p (c n) -> p c n", c=FC)
        wqk = node[:, 6144:6656].rearrange("p (c n) -> p c n", c=FC)
        attT = node[:, 6656:7808].rearrange("p (t n) -> p t n", t=NT)
        qT = node[0:D0, 7808:8192]
        kT = node[0:D0, 8192:8576]
        yT = node[:, 4096:7168].rearrange("p (g n) -> p g n", g=REL * FC)
        gx = node[:, 7168:10240].rearrange("p (r t n) -> p r t n", r=REL, t=NT)
        oh = node[:, 8576:10304].bitcast(BF16)
        oh_s = oh[:, 0:EB * 2 * N].rearrange("p (k n) -> p k n", k=EB)
        oh_d = oh[:, EB * 2 * N:EB * 3 * N].rearrange("p (k n) -> p k n", k=EB)

        x = sb("x", [P, NT, F])
        h = sb("h", [P, NT, F])
        hT = sb("hT", [P, FC, N])
        att = h[:, :, 0:N]
        rows = sb("rows", [P, 3, F])
        deg_row = sb("deg_row", [P, N])

        iota32 = sb("iota32", [P, N])
        iota16 = sb("iota16", [P, N], F16)
        pidx = sb("pidx", [P, 1])
        ident = sb("ident", [P, P])
        ones = sb("ones", [P, P])
        edge_i = sb("edge_i", [P, 3, ET], I32)
        src_f = sb("src_f", [P, ET])
        src0_f = sb("src0_f", [P, ET])
        dst_f = sb("dst_f", [P, ET])
        typ0 = sb("typ0", [P, ET])
        mixc = sb("mixc", [P, 2, BASES, REL])
        gw = sb("gw", [P, 2, FC, REL])
        bqk = sb("bqk", [D0, 2])
        stats = sb("stats", [P, NT, 6])
        mv = sb("mv", [P, NT, 2])
        ve = sb("ve", [P, NT])
        lnv = sb("lnv", [P, NT])
        y0 = sb("y0", [P, NT])
        y1 = sb("y1", [P, NT])
        rstd = sb("rstd", [P, NT])
        nbias = sb("nbias", [P, NT])
        hsum = sb("hsum", [P, FC])
        v7 = sb("v7", [P, NT, D0])
        smax = sb("smax", [P, NT])
        ssum = sb("ssum", [P, NT])
        srec = sb("srec", [P, NT])
        gate = sb("gate", [P, NT, REL])

        W1O, W2O = 18432, 10240
        ga_w = [mixm[:, 10240:14336].rearrange("p (c n) -> p c n", c=FC),
                mixm[:, 0:4096].rearrange("p (c n) -> p c n", c=2 * FC)]
        ga_wT = [mixm[:, 14336:18432].rearrange("p (j n) -> p j n", j=HEADS),
                 mixm[:, 4096:8192].rearrange("p (j n) -> p j n", j=FC)]
        ga_b = mixm[:, 8192:9728]
        C = [C1, C2]
        hx = [node[:, 0:NT * HEADS * (c + 1)].rearrange("p (t h n) -> p t h n", t=NT, h=HEADS) for c in C]
        o_ga = [node[:, 3096:6168].rearrange("p (t n) -> p t n", t=NT),
                node[:, 1560:3096].rearrange("p (t n) -> p t n", t=NT)]
        oT = node[:, 6168:9240].rearrange("p (c n) -> p c n", c=2 * FC)
        far = node[:, 9240:10392].rearrange("p (t n) -> p t n", t=NT)
        wa = [sb("wa0", [P, FC, 40]), sb("wa1", [P, 2 * FC, 40])]
        ga_a = [sb("ga_a0", [P, HEADS, 2]), sb("ga_a1", [P, 2, FC, 2])]
        aT = sb("aT", [40, N])
        rT = sb("rT", [40, N])
        acols = sb("acols", [P, NT, 40])
        rcols = sb("rcols", [P, NT, 40])
        far_max = sb("far_max", [P, NT, HEADS])
        far_m = sb("far_m", [P, NT, HEADS])
        as02 = sb("as02", [P, NT, HEADS])
        den = sb("den", [P, 2, NT])
        rec = sb("rec", [P, 2, NT])
        lsum = sb("lsum", [P, NT])
        lmax = sb("lmax", [P, NT])

        w_hh = mixm[:, 18432:24576].rearrange("p (c n) -> p c n", c=FC)
        w1a = mixm[:, 24576:26624].rearrange("p (c n) -> p c n", c=FC)
        w_ih = mixm[:, 10240:16384].rearrange("p (c n) -> p c n", c=FC)
        w2 = mixm[:, 16384:18432].rearrange("p (c n) -> p c n", c=FC)
        w1b = sb("w1b", [P, F])
        b_hh = rows[:].rearrange("p a n -> p (a n)")
        b_ih = mixm[:, 8192:9728]
        b1 = mixm[:, 9728:10240]
        agg = mixm[:, 0:1536].rearrange("p (t n) -> p t n", t=NT)
        aggT = mixm[:, 1536:3072].rearrange("p (c n) -> p c n", c=FC)
        mT = mixm[:, 4096:5632].rearrange("p (c n) -> p c n", c=FC)
        bn_rows = mixm[:, 5632:6656].rearrange("p (a n) -> p a n", a=2)
        gh = node[:, 0:4608].rearrange("p (t n) -> p t n", t=NT)
        got = node[:, 4608:9216].rearrange("p (q n) -> p q n", q=LB)
        ea = node[:, 9216:10368].rearrange("p (m n) -> p m n", m=LB // LC)
        tmp = node[:, 4608:9216].rearrange("p (q n) -> p q n", q=LB)
        idx = sb("idx", [P, LB // LC, LC], I32)
        pool_mark = sb("pool_mark", [P, 1])
        bn = sb("bn", [P, 5, FC])
        bn_ve = sb("bn_ve", [P, FC])
        bn_y0 = sb("bn_y0", [P, FC])
        bn_y1 = sb("bn_y1", [P, FC])
        bn_s = sb("bn_s", [P, 2, FC])
        with nc.sbuf_tensor("mats", [P, 4, NT, N], F32) as mats:
            cnt, cntT, c0T, c1T = (mats[:, i] for i in range(4))
        m_hi = sb("m_hi", [P, 3, F], F32R)
        m_lo = sb("m_lo", [P, 3, F], F32R)
        oh_r = sb("oh_r", [P, 3, N], F32R)
        ex = mats[:, 1:4]
        nodes_dram = nc.dram_tensor("nodes_scratch", (N, F), F32, kind="Internal").ap()

        ld_x, ld_edge, ld_l0, ld_mixc, ld_l1 = (sem(f"ld_{n}") for n in ("x", "edge", "l0", "mixc", "l1"))
        ld_v = [sem(f"ld_v{k}") for k in range(4)]
        ld_g = [sem(f"ld_g{k}") for k in range(2)]
        out_sem = sem("out_sem")
        consts = sem("consts")
        ident_ok = sem("ident_ok")
        v_step = sem("v_step")
        s_step = sem("s_step")
        ln_var = sem("ln_var")
        ln_y = sem("ln_y")
        ln_scale = sem("ln_scale")
        h_ok = sem("h_ok")
        hT_mm = sem("hT_mm")
        hT_v = sem("hT_v")
        hT_s = sem("hT_s")
        hsum_ok = sem("hsum_ok")
        l0_mm = sem("l0_mm")
        qk_ok = sem("qk_ok")
        v_ok = sem("v_ok")
        oh_ok = sem("oh_ok")
        oh_used = sem("oh_used")
        cnt_ok = sem("cnt_ok")
        cntn_mm = sem("cntn_mm")
        cntn_ok = sem("cntn_ok")
        deg_mm = sem("deg_mm")
        deg_ok = sem("deg_ok")
        sc_mm = sem("sc_mm")
        sc_ok = sem("sc_ok")
        ex_ok = sem("ex_ok")
        attT_mm = sem("attT_mm")
        attT_ok = sem("attT_ok")
        o7_mm = sem("o7_mm")
        gate_mm = sem("gate_mm")
        gate_ok = sem("gate_ok")
        gx_ok = sem("gx_ok")
        yT_mm = sem("yT_mm")
        yT_v = sem("yT_v")
        w_ok = sem("w_ok")
        rg_mm = sem("rg_mm")
        h2_ok = sem("h2_ok")
        mix_done = sem("mix_done")
        prod_ok = sem("prod_ok")
        prod_added = sem("prod_added")
        x2_ok = sem("x2_ok")
        ld_ga = [sem("ld_ga0"), sem("ld_ga1")]
        ld_gaT = [sem("ld_gaT0"), sem("ld_gaT1")]
        ld_gab = sem("ld_gab")
        ld_l3 = sem("ld_l3")
        ld_ih = sem("ld_ih")
        ld_b3 = sem("ld_b3")
        ld_ea = [sem(f"ld_ea{m}") for m in range(LB // LC)]
        ld_got = [sem(f"ld_got{q}") for q in range(LB)]
        set_ok = sem("set_ok")
        wa_mm = sem("wa_mm")
        wa_ok = sem("wa_ok")
        aT_mm = sem("aT_mm")
        aT_ok = sem("aT_ok")
        ac_mm = sem("ac_mm")
        ac_ok = sem("ac_ok")
        as_mm = sem("as_mm")
        far_ok = sem("far_ok")
        hx_mm = sem("hx_mm")
        hx_ok = sem("hx_ok")
        rc_ok = sem("rc_ok")
        rT_mm = sem("rT_mm")
        rT_ok = sem("rT_ok")
        rb_mm = sem("rb_mm")
        low_ok = sem("low_ok")
        lr_ok = sem("lr_ok")
        exg_ok = sem("exg_ok")
        pg_ok = sem("pg_ok")
        pv_mm = sem("pv_mm")
        pv_used = sem("pv_used")
        oT_mm = sem("oT_mm")
        oT_v = sem("oT_v")
        oT_s = sem("oT_s")
        ls_max = sem("ls_max")
        ls_sum = sem("ls_sum")
        bn_var = sem("bn_var")
        bn_y = sem("bn_y")
        bn_ok = sem("bn_ok")
        bnr_mm = sem("bnr_mm")
        pn_mm = sem("pn_mm")
        pn_ok = sem("pn_ok")
        pn_st = sem("pn_st")
        gh_mm = sem("gh_mm")
        gh_ok = sem("gh_ok")
        marks = sem("marks")
        pre_mm = sem("pre_mm")
        sum_ok = sem("sum_ok")
        hi_ok = sem("hi_ok")
        lo_ok = sem("lo_ok")
        scat = sem("scat")
        agg_v = sem("agg_v")
        aggT_mm = sem("aggT_mm")
        aggT_ok = sem("aggT_ok")
        mT_mm = sem("mT_mm")
        mT_ok = sem("mT_ok")
        gi_mm = sem("gi_mm")
        gs_v = sem("gs_v")
        gs_s = sem("gs_s")
        gn_v = sem("gn_v")
        gn_s = sem("gn_s")
        out_ok = sem("out_ok")

        bank = [ps[:, b, :] for b in range(8)]

        def bank3(b, w):
            return bank[b][:, 0:NT * w].rearrange("p (t n) -> p t n", t=NT)

        def cols(t):
            return slice(t * P, (t + 1) * P)

        def load_mix_v(eng, u, k):
            eng.dma_start(ring_v[:, k:k + 1, :], a["basis_v"][:, bass.ds(u, 1), :]).then_inc(ld_v[k], 16)

        def load_mix_g(eng, u, k):
            eng.dma_start(ring_g[:, k:k + 1, :], a["basis_g"][:, bass.ds(u, 1), :]).then_inc(ld_g[k], 16)

        YB = [5, 6, 7, 0, 1, 2, 3, 4]

        def hx_banks(g):
            return ([0, 1, 2], 1) if g else ([0, 1, 2, 3, 6, 7], 2)

        grz = tmp[:, 0:4, :].rearrange("p (b a) n -> p b (a n)", b=2)
        gn = tmp[:, 4:6, :]
        gd = tmp[:, 6:8, :]
        GB = [1, 2, 3, 1, 2, 3, 1, 2, 3]

        block = ctx.enter_context(nc.Block())

        @block.sync
        def _(sp):
            sp.dma_start(x[:], a["x"]).then_inc(ld_x, 16)
            sp.dma_start(edge_i[:], a["edge"]).then_inc(ld_edge, 16)
            sp.dma_start(wqk, a["wqk"]).then_inc(ld_l0, 16)
            sp.dma_start(bqk[:], a["bqk"]).then_inc(ld_l0, 16)
            sp.dma_start(wv, a["wv"]).then_inc(ld_l0, 16)
            sp.dma_start(rows[:], a["rows"].partition_broadcast(P)).then_inc(ld_l0, 16)
            sp.dma_start(mixc[:], a["mixc"].partition_broadcast(P)).then_inc(ld_mixc, 16)
            for k in range(2):
                load_mix_v(sp, k, k)
            sp.dma_start(ga_a[0][:], a["ga_a1"]).then_inc(ld_gab, 16)
            sp.wait_ge(set_ok, 1)
            for e in range(2):
                sp.dma_start(ga_a[1][e * C2:(e + 1) * C2, e], a["ga_a2"][:, e]).then_inc(ld_gab, 16)
            sp.dma_start(gw[:], a["gw"]).then_inc(ld_l1, 16)
            sp.dma_start(roots, a["roots"]).then_inc(ld_l1, 16)

            with sp.Fori(1, CT) as i:
                for k in range(2):
                    sp.wait_ge(mix_done, i * 4 + (2 * k - 2))
                    load_mix_v(sp, i * 2 + k, k)

            def mix_loads(i0, i1):
                with sp.Fori(i0, i1) as i:
                    for k in range(4):
                        sp.wait_ge(mix_done, i * 8 + (2 * k - 6))
                        load_mix_v(sp, i * 4 + k, k)

            for k in range(4):
                if k < 2:
                    sp.wait_ge(mix_done, 4 * CT + 2 * k - 2)
                load_mix_v(sp, 2 * CT + k, k)
            mix_loads(CT // 2 + 1, UV // 4 + 1)
            sp.wait_ge(w_ok, 4)
            sp.dma_start(ga_w[0], a["ga_w1"]).then_inc(ld_ga[0], 16)
            mix_loads(UV // 4 + 1, UV // 4 + 4)
            sp.wait_ge(rg_mm, NT)
            sp.dma_start(ga_wT[0], a["ga_w1T"]).then_inc(ld_gaT[0], 16)
            mix_loads(UV // 4 + 4, 2 * UV // 4)
            sp.wait_ge(mix_done, 2 * 2 * UV)
            sp.dma_start(ga_w[1], a["ga_w2"]).then_inc(ld_ga[1], 16)
            sp.wait_ge(prod_added, 2 * 2 * UG)
            sp.dma_start(ga_wT[1], a["ga_w2T"]).then_inc(ld_gaT[1], 16)
            sp.dma_start(ga_b, a["ga_b"].partition_broadcast(P)).then_inc(ld_gab, 16)
            sp.dma_start(b1, a["b1"].partition_broadcast(P)).then_inc(ld_l3, 16)
            sp.dma_start(w1b[:], a["w1b"]).then_inc(ld_l3, 16)
            sp.dma_start(bn[:], a["bn"]).then_inc(ld_l3, 16)
            sp.wait_ge(rg_mm, 2 * NT)
            sp.dma_start(w1a, a["w1a"]).then_inc(ld_l3, 16)
            sp.dma_start(w_hh, a["w_hh"]).then_inc(ld_l3, 16)
            sp.wait_ge(x2_ok, NT)
            sp.dma_start(b_hh, a["b_hh"].partition_broadcast(P)).then_inc(ld_l3, 16)
            sp.wait_ge(hx_mm, 2 * NT)
            sp.dma_start(w_ih, a["w_ih"]).then_inc(ld_ih, 16)
            sp.dma_start(w2, a["w2"]).then_inc(ld_ih, 16)
            sp.wait_ge(pv_used, 2 * HEADS)
            sp.dma_start(b_ih, a["b_ih"].partition_broadcast(P)).then_inc(ld_b3, 16)
            sp.wait_ge(ls_sum, 1)

            def edges(i, first):
                for m in range(LB // LC):
                    if not first:
                        sp.wait_ge(sum_ok, i * LB + (LC * m - LB + LC))
                    at = bass.ds(i * (LB // LC) + m, 1)
                    sp.dma_start(ea[:, m:m + 1, :], a["edge_attr"][:, at, :]).then_inc(ld_ea[m], 16)
                    sp.dma_start(idx[:, m:m + 1, :], a["src_idx"][:, at, :]).then_inc(ld_ea[m], 16)

            edges(0, True)
            sp.wait_ge(pn_ok, NT)
            sp.dma_start(nodes_dram.rearrange("(t p) n -> p t n", p=P), agg).then_inc(pn_st, 16)
            with sp.Fori(1, ET // LB) as i:
                edges(i, False)
            for t in range(NT):
                sp.wait_ge(out_ok, t + 1)
                sp.dma_start(out[:, t, :], x[:, t, :]).then_inc(out_sem, 16)
            sp.wait_ge(out_sem, 16 * NT)

        @block.gpsimd
        def _(pool):
            nc.gpsimd.iota(iota32[:], [[1, N]], base=0, channel_multiplier=0,
                           allow_small_or_imprecise_dtypes=True)
            nc.gpsimd.iota(iota16[:], [[1, N]], base=0, channel_multiplier=0,
                           allow_small_or_imprecise_dtypes=True)
            nc.gpsimd.iota(pidx[:], [[0, 1]], base=0, channel_multiplier=1,
                           allow_small_or_imprecise_dtypes=True).then_inc(consts, 1)

            def add_product(layer, p, k, r, first):
                pool.wait_ge(prod_ok, p + 1)
                acc = quarter(acc_g[layer], r, k)
                if first:
                    nc.gpsimd.tensor_copy(acc, prod[:, k, r, :]).then_inc(prod_added, 1)
                else:
                    pool.wait_ge(prod_added, p - 3)
                    nc.gpsimd.tensor_tensor(acc, acc, prod[:, k, r, :], ALU.add).then_inc(prod_added, 1)

            for layer in range(2):
                for k in range(2):
                    for r in range(REL):
                        add_product(layer, layer * 2 * UG + 2 * k + r, k, r, True)
                with pool.Fori(layer * UG // 2 + 1, (layer + 1) * UG // 2) as i:
                    for k in range(2):
                        for r in range(REL):
                            add_product(layer, i * 4 + (2 * k + r), k, r, False)

            for n in range(2 * HEADS):
                pool.wait_ge(exg_ok, n + 1)
                hd = n % HEADS
                nc.gpsimd.tensor_tensor(ex[:, hd % 3], ex[:, hd % 3], cnt, ALU.mult).then_inc(pg_ok, 1)

            nc.gpsimd.memset(pool_mark[:], 0.0).then_inc(marks, 1)
            pool.wait_ge(pn_st, 16)

            def mark(n):
                pool.wait_ge(marks, n)
                nc.gpsimd.tensor_tensor(pool_mark[:], pool_mark[:], pool_mark[:], ALU.add).then_inc(marks, 1)

            def gathers(i, first):
                n = 1 if first else i * (LB + LB // LC) + (1 - LB)
                for q in range(LB):
                    if q % LC == 0:
                        pool.wait_ge(ld_ea[q // LC], i * 32 + 32)
                        mark(n)
                        n = n + 1
                    if not first:
                        pool.wait_ge(lo_ok, i * LB + (q - LB + 1))
                        mark(n)
                        n = n + 1
                    nc.gpsimd.indirect_dma_start(
                        out=got[:, q, :], out_offset=None, in_=nodes_dram,
                        in_offset=bass.IndirectOffsetOnAxis(ap=idx[:, q // LC, q % LC:q % LC + 1], axis=0)
                    ).then_inc(ld_got[q], 16)

            gathers(0, True)
            with pool.Fori(1, ET // LB) as i:
                gathers(i, False)

        @block.scalar
        def _(act):
            def ln_act(s, before=None):
                act.wait_ge(ln_var, s + 1)
                nc.scalar.activation(lnv[:], ve[:], ACT.Ln).then_inc(s_step, 1)
                act.wait_ge(s_step, (s if before is None else before) + 1)
                nc.scalar.activation(y0[:], lnv[:], ACT.Exp, scale=-0.5).then_inc(ln_y, 1)
                act.wait_ge(ln_scale, s + 1)
                for t in range(NT):
                    nc.scalar.activation(h[:, t, :], x[:, t, :], ACT.Relu, bias=nbias[:, t:t + 1],
                                         scale=rstd[:, t:t + 1]).then_inc(h_ok, 1)

            def hT_act(s):
                for c in (1, 3):
                    act.wait_ge(hT_mm, FC * s + c + 1)
                    nc.scalar.copy(hT[:, c, :], bank[c][:, 0:N]).then_inc(hT_s, 1)

            flat = mixc[:].rearrange("p l b r -> p (l b) r")

            def products(layer, i0, i1):
                base = layer * BASES + MIX_V

                def turn(i, first, last):
                    def operands(k):
                        act.wait_ge(ld_g[k], (i + 1) * 16)
                        if not first:
                            act.wait_ge(prod_added, i * 4 + (2 * k - 2))

                    operands(0)
                    for k in range(2):
                        for r in range(REL):
                            nc.scalar.activation(prod[:, k, r, :], ring_g[:, k, :], ACT.Copy,
                                                 scale=flat[:, bass.ds(i + (base - layer * MIX_G), 1), r]
                                                 ).then_inc(prod_ok, 1)
                        if k == 0:
                            operands(1)
                        if not last:
                            act.wait_ge(prod_ok, i * 4 + (2 * k + 2))
                            load_mix_g(act, i * 2 + (2 + k), k)

                if i0 == 0:
                    for k in range(2):
                        load_mix_g(act, k, k)
                    act.wait_ge(ld_mixc, 16)
                    turn(0, True, False)
                last = i1 == 2 * MIX_G
                if i1 - last > max(i0, 1):
                    with act.Fori(max(i0, 1), i1 - last) as i:
                        turn(i, False, False)
                if last:
                    turn(2 * MIX_G - 1, False, True)

            def relational_act(l):
                act.wait_ge(gate_mm, l + 1)
                nc.scalar.activation(gate[:], bank3(4, REL), ACT.Sigmoid).then_inc(gate_ok, 1)

            ln_act(0)
            hT_act(0)
            act.wait_ge(ld_l0, 64)
            for n, (t_, b) in enumerate(((qT, 4), (kT, 5))):
                act.wait_ge(l0_mm, n + 1)
                nc.scalar.activation(t_, bank[b][0:D0, 0:N], ACT.Identity,
                                     bias=bqk[:, n:n + 1]).then_inc(qk_ok, 1)
            products(0, 0, MIX_G)
            for t in range(NT):
                act.wait_ge(sc_ok, t + 1)
                nc.scalar.activation(att[:, t, :], att[:, t, :], ACT.Exp, bias=smax[:, t:t + 1],
                                     accum_out=ssum[:, t:t + 1]).then_inc(ex_ok, 1)
            products(1, MIX_G, MIX_G + 1)
            ln_act(1)
            products(1, MIX_G + 1, MIX_G + 2)
            relational_act(0)
            products(1, MIX_G + 2, MIX_G + 7)
            relational_act(1)
            products(1, MIX_G + 7, 2 * MIX_G)
            act.wait_ge(set_ok, 1)
            for g in range(2):
                act.wait_ge(wa_mm, g + 1)
                kc = FC * (g + 1)
                v = bank[g][:, 0:kc * 16].rearrange("p (c e n) -> p c e n", c=kc, e=2)
                for e in range(2):
                    ins = nc.scalar.copy(wa[g][:, :, 32 * e:32 * e + 8], v[:, :, e, :])
                ins.then_inc(wa_ok, 1)

            def attention_act(g):
                nh = C[g]
                act.wait_ge(aT_mm, g + 1)
                nc.scalar.copy(aT[:], bank[4][0:40, 0:N]).then_inc(aT_ok, 1)
                banks, per = hx_banks(g)
                for n, b in enumerate(banks):
                    t, part = divmod(n, per)
                    act.wait_ge(hx_mm, (2 * NT if g else 0) + n + 1)
                    heads = HEADS // per
                    nc.scalar.copy(hx[g][:, t, part * heads:(part + 1) * heads, 0:nh],
                                   bank[b].rearrange("p (h n) -> p h n", h=heads)).then_inc(hx_ok, 1)

                def low(hd):
                    n = g * HEADS + hd
                    act.wait_ge(rb_mm, 2 * n + 2)
                    if n >= 3:
                        act.wait_ge(pv_mm, g * HEADS + max(hd - 2, 0))
                    for t in range(NT):
                        nc.scalar.activation(ex[:, hd % 3, t, :], bank[6 + hd % 2][:, 0:N], ACT.Identity,
                                             bias=as02[:, t, hd:hd + 1]).then_inc(low_ok, 1)

                low(0)
                low(1)
                for hd in range(HEADS):
                    act.wait_ge(lr_ok, g * HEADS + hd + 1)
                    nc.scalar.activation(ex[:, hd % 3], ex[:, hd % 3], ACT.Exp).then_inc(exg_ok, 1)
                    if hd + 2 < HEADS:
                        low(hd + 2)

            ln_act(2)
            hT_act(3)
            attention_act(0)
            for c in range(1, 2 * FC, 2):
                act.wait_ge(oT_mm, c + 1)
                nc.scalar.activation(oT[:, c, :], bank[c][:, 0:N], ACT.Relu).then_inc(oT_s, 1)
            attention_act(1)
            act.wait_ge(ls_max, 1)
            for t in range(NT):
                ins = nc.scalar.activation(tmp[:, t, :], o_ga[1][:, t, :], ACT.Exp, bias=lmax[:, t:t + 1],
                                           accum_out=lsum[:, t:t + 1])
            ins.then_inc(s_step, 1)
            act.wait_ge(s_step, 4)
            nc.scalar.activation(lsum[:], lsum[:], ACT.Ln).then_inc(ls_sum, 1)
            act.wait_ge(bn_var, 1)
            nc.scalar.activation(bn_y0[:], bn_ve[:], ACT.Ln).then_inc(s_step, 1)
            act.wait_ge(s_step, 5)
            nc.scalar.activation(bn_y0[:], bn_y0[:], ACT.Exp, scale=-0.5).then_inc(bn_y, 1)
            ln_act(3, 5)
            hT_act(4)

            def upper(i, first):
                for q in range(LB):
                    act.wait_ge(sum_ok, i * LB + (q + 1))
                    if not (first and q < 3):
                        act.wait_ge(scat, i * LB + (q - 2))
                    nc.scalar.activation(m_hi[:, q % 3, :], got[:, q, :], ACT.Relu).then_inc(hi_ok, 1)

            upper(0, True)
            with act.Fori(1, ET // LB) as i:
                upper(i, False)
            for t in range(NT):
                act.wait_ge(gs_v, t + 1)
                nc.scalar.activation(grz[:, t % 2], grz[:, t % 2], ACT.Sigmoid).then_inc(gs_s, 1)
                act.wait_ge(gn_v, t + 1)
                nc.scalar.activation(gn[:, t % 2], gn[:, t % 2], ACT.Tanh).then_inc(gn_s, 1)

        @block.vector
        def _(dve):
            steps = [0]

            def link(ins):
                steps[0] += 1
                ins.then_inc(v_step, 1)
                dve.wait_ge(v_step, steps[0])

            def ln_vec(s):
                for t in range(NT):
                    ins = nc.vector.bn_stats(stats[:, t, :], x[:, t, :])
                link(ins)
                for t in range(NT):
                    ins = nc.vector.bn_aggr(mv[:, t, :], stats[:, t, :])
                link(ins)
                nc.vector.tensor_scalar(ve[:], mv[:, :, 1], LN_EPS, None, ALU.add).then_inc(ln_var, 1)
                dve.wait_ge(ln_y, s + 1)
                link(nc.vector.tensor_tensor(y1[:], y0[:], y0[:], ALU.mult))
                link(nc.vector.tensor_tensor(y1[:], y1[:], ve[:], ALU.mult))
                link(nc.vector.tensor_scalar(y1[:], y1[:], -0.5, 1.5, ALU.mult, ALU.add))
                link(nc.vector.tensor_tensor(rstd[:], y0[:], y1[:], ALU.mult))
                nc.vector.scalar_tensor_tensor(out=nbias[:], in0=mv[:, :, 0], scalar=-1.0, in1=rstd[:],
                                               op0=ALU.mult, op1=ALU.mult).then_inc(ln_scale, 1)

            def hT_vec(s):
                for c in (range(FC) if s in (1, 2) else (0, 2)):
                    dve.wait_ge(hT_mm, FC * s + c + 1)
                    nc.vector.tensor_copy(hT[:, c, :], bank[c][:, 0:N]).then_inc(hT_v, 1)

            flat = mixc[:].rearrange("p l b r -> p (l b) r")

            def mix_unit(layer, u, k, half, landed, first=False):
                dve.wait_ge(ld_v[k], landed)
                base = layer * (BASES - MIX_V)
                b = u // 2 if isinstance(u, int) else u[0]
                u = u if isinstance(u, int) else u[1]
                for r in range(REL):
                    acc = quarter(w_mix[layer], r, half)
                    scale = flat[:, bass.ds(b + base, 1), r]
                    if first:
                        nc.vector.tensor_scalar(acc, ring_v[:, k, :], scale, None, ALU.mult).then_inc(mix_done, 1)
                    else:
                        dve.wait_ge(mix_done, u * 2 + (r - 3))
                        nc.vector.scalar_tensor_tensor(out=acc, in0=ring_v[:, k, :], scalar=scale, in1=acc,
                                                       op0=ALU.mult, op1=ALU.add).then_inc(mix_done, 1)

            def landed(u):
                return 16 * (u // 2 + 1) if u < 2 * CT else 16 * ((CT if u % 4 < 2 else 0) + u // 4 - CT // 2 + 1)

            mixed = [2 * CT]

            def mix(n):
                u0, u1 = mixed[0], mixed[0] + n
                mixed[0] = u1
                layer = u0 // UV
                u = u0
                while u < u1:
                    if u % 4 == 0 and u1 - u >= 8 and u % UV >= 2:
                        turns = (u1 - u) // 4
                        with dve.Fori(u // 4, u // 4 + turns) as i:
                            for k in range(4):
                                mix_unit(layer, (i * 2 + k // 2, i * 4 + k), k, k % 2,
                                         i * 16 + (landed(k + 2 * CT) - 16 * (CT // 2)))
                        u += 4 * turns
                    else:
                        mix_unit(layer, u, u % 4, u % 2, landed(u), first=u % UV < 2)
                        u += 1

            def merge(layer):
                dve.wait_ge(prod_added, (layer + 1) * 2 * UG)
                dve.wait_ge(mix_done, (layer + 1) * 2 * UV)
                for r in range(REL):
                    for half in range(2):
                        w = quarter(w_mix[layer], r, half)
                        nc.vector.tensor_tensor(w, w, quarter(acc_g[layer], r, half), ALU.add).then_inc(w_ok, 1)

            def relational_vec(l):
                dve.wait_ge(gate_ok, l + 1)
                for r in range(REL):
                    for t in range(NT):
                        nc.vector.tensor_scalar(gx[:, r, t, :], h[:, t, :], gate[:, t, r:r + 1], None,
                                                ALU.mult).then_inc(gx_ok, 1)
                for g in range(REL * FC):
                    if g % 2 == 0:
                        mix(1)
                    dve.wait_ge(yT_mm, REL * FC * l + g + 1)
                    nc.vector.tensor_copy(yT[:, g, :], bank[YB[g]][:, 0:N]).then_inc(yT_v, 1)

            for t_ in (wa[0], wa[1], ga_a[1], rcols):
                ins = nc.vector.memset(t_[:], 0.0)
            ins.then_inc(set_ok, 1)
            dve.wait_ge(consts, 1)
            nc.vector.memset(ones[:], 1.0)
            nc.vector.tensor_scalar(ident[:], iota32[:, 0:P], pidx[:, 0:1], None,
                                    ALU.is_equal).then_inc(ident_ok, 1)
            dve.wait_ge(ld_edge, 16)
            nc.vector.tensor_copy(src_f[:], edge_i[:, 0, :])
            nc.vector.tensor_copy(dst_f[:], edge_i[:, 1, :])
            nc.vector.tensor_copy(typ0[:], edge_i[:, 2, :])
            link(nc.vector.memset(hsum[:], 0.0))
            link(nc.vector.tensor_scalar(typ0[:], typ0[:], 0.0, None, ALU.is_equal))
            link(nc.vector.scalar_tensor_tensor(out=src0_f[:], in0=src_f[:], scalar=1.0, in1=typ0[:],
                                                op0=ALU.add, op1=ALU.mult))
            link(nc.vector.tensor_scalar(src0_f[:], src0_f[:], -1.0, None, ALU.add))
            dve.wait_ge(ld_x, 16)
            ln_vec(0)
            hT_vec(0)
            dve.wait_ge(hT_v, 2)
            dve.wait_ge(hT_s, 2)
            nc.vector.reduce_sum(hsum[:], hT[:], AX_X).then_inc(hsum_ok, 1)
            dve.wait_ge(ld_l0, 64)
            dve.wait_ge(l0_mm, 3)
            for t in range(NT):
                nc.vector.tensor_tensor(v7[:, t, :], bank3(6, D0)[:, t, :], rows[:, 0, F - D0:F], ALU.add)
            dve.wait_ge(l0_mm, 4)
            mean = gx[:, 0, 0, 0:F - D0]
            link(nc.vector.scalar_tensor_tensor(out=mean, in0=bank[7][:, 0:F - D0], scalar=1.0 / N,
                                                in1=rows[:, 0, 0:F - D0], op0=ALU.mult, op1=ALU.add))
            dve.wait_ge(h_ok, NT)
            for t in range(NT):
                ins = nc.vector.tensor_tensor(x[:, t, 0:F - D0], x[:, t, 0:F - D0], mean, ALU.add)
            ins.then_inc(v_ok, 1)

            def one_hots(i, first, tiles=CB):
                for q in range(tiles):
                    k = q % EB
                    if not (first and q < EB):
                        dve.wait_ge(oh_used, i * CB + (q - EB + 1))
                    at = bass.ds(i * CB + q, 1)
                    nc.vector.tensor_scalar(oh_d[:, k, :], iota16[:], dst_f[:, at], None, ALU.is_equal)
                    nc.vector.tensor_scalar(oh_s[:, k, 0:N], iota16[:], src_f[:, at], None, ALU.is_equal)
                    nc.vector.tensor_scalar(oh_s[:, k, N:2 * N], iota16[:], src0_f[:, at], None,
                                            ALU.is_equal).then_inc(oh_ok, 1)
                    if q in (tiles // 3, 2 * tiles // 3):
                        e = 0 if q == tiles // 3 else 1
                        mix_unit(0, i * 2 + e if isinstance(i, int) else (i, i * 2 + e), e, e, i * 16 + 16, first)

            dve.wait_ge(ld_mixc, 16)
            one_hots(0, True)
            with dve.Fori(1, CT - 1) as i:
                one_hots(i, False)
            one_hots(CT - 1, False, ET - CB * (CT - 1))
            dve.wait_ge(oh_used, ET)
            for j in range(NT):
                nc.vector.tensor_copy(cntT[:, j, :], bank[j][:, 0:N]).then_inc(cnt_ok, 1)
            for j in range(NT):
                nc.vector.tensor_copy(c0T[:, j, :], bank[3 + j][:, 0:N]).then_inc(cnt_ok, 1)
            dve.wait_ge(cnt_ok, 2 * NT)
            nc.vector.tensor_tensor(c1T[:], cntT[:], c0T[:], ALU.subtract).then_inc(cnt_ok, 1)
            for t in range(NT):
                dve.wait_ge(cntn_mm, t + 1)
                nc.vector.tensor_copy(cnt[:, t, :], bank[t][:, 0:N]).then_inc(cntn_ok, 1)
            dve.wait_ge(cntn_ok, NT)
            for t in range(NT):
                ins = nc.vector.tensor_scalar(att[:, t, :], cnt[:, t, :], 0.5, None, ALU.is_gt)
            link(ins)
            for t in range(NT):
                dve.wait_ge(sc_mm, t + 1)
                link(nc.vector.scalar_tensor_tensor(out=att[:, t, :], in0=bank[3 + t][:, 0:N],
                                                    scalar=float(D0) ** -0.5, in1=att[:, t, :],
                                                    op0=ALU.mult, op1=ALU.mult))
                link(nc.vector.reduce_max(smax[:, t:t + 1], att[:, t, :], AX_X))
                nc.vector.tensor_scalar(smax[:, t:t + 1], smax[:, t:t + 1], -1.0, None,
                                        ALU.mult).then_inc(sc_ok, 1)
            mix(1)
            dve.wait_ge(deg_mm, 1)
            nc.vector.tensor_copy(deg_row[:], bank[6][:, 0:N]).then_inc(deg_ok, 1)
            for j in range(NT):
                dve.wait_ge(attT_mm, j + 1)
                nc.vector.tensor_copy(attT[:, j, :], bank[j][:, 0:N]).then_inc(attT_ok, 1)
            dve.wait_ge(ex_ok, NT)
            link(nc.vector.reciprocal(srec[:], ssum[:]))
            mix(1)
            dve.wait_ge(o7_mm, 1)
            for t in range(NT):
                ins = nc.vector.scalar_tensor_tensor(out=x[:, t, F - D0:F], in0=bank3(7, D0)[:, t, :],
                                                     scalar=srec[:, t:t + 1], in1=x[:, t, F - D0:F],
                                                     op0=ALU.mult, op1=ALU.add)
            link(ins)
            ln_vec(1)
            hT_vec(1)
            relational_vec(0)
            for t in range(NT):
                nc.vector.tensor_tensor(x[:, t, :], x[:, t, :], rows[:, 2, :], ALU.add)
            mix(UV - mixed[0])
            merge(0)
            mix(6)
            for t in range(NT):
                dve.wait_ge(rg_mm, t + 1)
                link(nc.vector.tensor_tensor(h[:, t, :], bank[5 + t], rows[:, 1, :], ALU.add))
                nc.vector.tensor_scalar(h[:, t, :], h[:, t, :], 0.0, None, ALU.max).then_inc(h2_ok, 1)
            hT_vec(2)
            relational_vec(1)
            mix(2 * UV - mixed[0])
            merge(1)
            for t in range(NT):
                dve.wait_ge(rg_mm, NT + t + 1)
                nc.vector.tensor_tensor(x[:, t, :], x[:, t, :], bank[5 + t], ALU.add).then_inc(x2_ok, 1)

            for t in range(NT):
                nc.vector.tensor_tensor(cnt[:, t, cols(t)], cnt[:, t, cols(t)], ident[:], ALU.add)
                ins = nc.vector.tensor_tensor(cntT[:, t, cols(t)], cntT[:, t, cols(t)], ident[:], ALU.add)
            link(ins)
            nc.vector.tensor_scalar(far, cntT, 0.5, FAR, ALU.is_lt, ALU.mult)
            nc.vector.memset(hx[0][:, :, :, C1], 1.0)
            dve.wait_ge(x2_ok, NT)
            ln_vec(2)
            hT_vec(3)

            def attention_vec(g):
                nh = C[g]
                done = g * HEADS
                dve.wait_ge(ac_mm, g + 1)
                nc.vector.tensor_copy(acols[:], bank3(5, 40)).then_inc(ac_ok, 1)
                for hd in range(HEADS):
                    dve.wait_ge(as_mm, done + hd + 1)
                    if hd >= 3:
                        dve.wait_ge(far_ok, done + hd - 2)
                    for j in range(NT):
                        ins = nc.vector.tensor_tensor_reduce(
                            out=ex[:, hd % 3, j, :], in0=bank[4 + hd % 2][:, 0:N], in1=far[:, j, :], scale=1.0,
                            scalar=2 * FAR, op0=ALU.add, op1=ALU.max, accum_out=far_max[:, j, hd:hd + 1])
                    ins.then_inc(far_ok, 1)
                dve.wait_ge(far_ok, done + HEADS)
                dve.wait_ge(ac_ok, g + 1)
                a_s, a_d = acols[:, :, 0:HEADS], acols[:, :, 32:40]
                nc.vector.tensor_scalar(as02[:], a_s, SLOPE, None, ALU.mult)
                link(nc.vector.tensor_tensor(far_m[:], far_max[:], a_d, ALU.add))
                link(nc.vector.scalar_tensor_tensor(out=far_m[:], in0=far_m[:], scalar=SLOPE, in1=far_m[:],
                                                    op0=ALU.mult, op1=ALU.max))
                nc.vector.tensor_tensor(rcols[:, :, 0:HEADS], a_d, far_m[:], ALU.subtract)
                nc.vector.scalar_tensor_tensor(out=rcols[:, :, 32:40], in0=a_d, scalar=SLOPE, in1=far_m[:],
                                               op0=ALU.mult, op1=ALU.subtract).then_inc(rc_ok, 1)
                dve.wait_ge(rT_mm, g + 1)
                nc.vector.tensor_copy(rT[:], bank[4][0:40, 0:N]).then_inc(rT_ok, 1)

                def leaky(hd):
                    n = done + hd
                    dve.wait_ge(rb_mm, 2 * n + 1)
                    for t in range(NT):
                        dve.wait_ge(low_ok, NT * n + t + 1)
                        ins = nc.vector.scalar_tensor_tensor(
                            out=ex[:, hd % 3, t, :], in0=bank[4 + hd % 2][:, 0:N], scalar=acols[:, t, hd:hd + 1],
                            in1=ex[:, hd % 3, t, :], op0=ALU.add, op1=ALU.max)
                    ins.then_inc(lr_ok, 1)

                def normalise(hd):
                    n = done + hd
                    dve.wait_ge(pv_mm, n + 1)
                    o = bank3(hd % 2, nh + 1)
                    link(nc.vector.tensor_scalar(den[:, hd % 2, :], o[:, :, nh], 1e-16, None, ALU.add))
                    link(nc.vector.reciprocal(rec[:, hd % 2, :], den[:, hd % 2, :]))
                    for j in range(NT):
                        ins = nc.vector.scalar_tensor_tensor(
                            out=o_ga[g][:, j, hd * nh:(hd + 1) * nh], in0=o[:, j, 0:nh],
                            scalar=rec[:, hd % 2, j:j + 1],
                            in1=ga_b[:, g * HEADS * C1 + hd * nh:g * HEADS * C1 + (hd + 1) * nh],
                            op0=ALU.mult, op1=ALU.add)
                    ins.then_inc(pv_used, 1)

                leaky(0)
                leaky(1)
                for hd in range(HEADS):
                    if hd + 2 < HEADS:
                        leaky(hd + 2)
                    normalise(hd)

            dve.wait_ge(ld_gab, 64)
            attention_vec(0)
            for c in range(0, 2 * FC, 2):
                dve.wait_ge(oT_mm, c + 1)
                nc.vector.tensor_scalar(oT[:, c, :], bank[c][:, 0:N], 0.0, None, ALU.max).then_inc(oT_v, 1)
            nc.vector.memset(hx[1][:, :, :, C2], 1.0).then_inc(set_ok, 1)
            attention_vec(1)
            dve.wait_ge(pv_used, 2 * HEADS)
            link(nc.vector.reduce_max(smax[:], o_ga[1], AX_X))
            nc.vector.tensor_scalar(lmax[:], smax[:], -1.0, None, ALU.mult).then_inc(ls_max, 1)
            dve.wait_ge(ld_l3, 96)
            nc.vector.tensor_scalar(bn_ve[:], bn[:, 3, :], BN_EPS, None, ALU.add).then_inc(bn_var, 1)
            dve.wait_ge(ls_sum, 1)
            link(nc.vector.tensor_tensor(lsum[:], smax[:], lsum[:], ALU.add))
            for t in range(NT):
                ins = nc.vector.scalar_tensor_tensor(out=x[:, t, :], in0=o_ga[1][:, t, :], scalar=lsum[:, t:t + 1],
                                                     in1=x[:, t, :], op0=ALU.subtract, op1=ALU.add)
            link(ins)
            ln_vec(3)
            hT_vec(4)
            dve.wait_ge(bn_y, 1)
            link(nc.vector.tensor_tensor(bn_y1[:], bn_y0[:], bn_y0[:], ALU.mult))
            link(nc.vector.tensor_tensor(bn_y1[:], bn_y1[:], bn_ve[:], ALU.mult))
            link(nc.vector.tensor_scalar(bn_y1[:], bn_y1[:], -0.5, 1.5, ALU.mult, ALU.add))
            link(nc.vector.tensor_tensor(bn_y1[:], bn_y1[:], bn_y0[:], ALU.mult))
            link(nc.vector.tensor_tensor(bn_s[:, 0, :], bn_y1[:], bn[:, 0, :], ALU.mult))
            link(nc.vector.tensor_tensor(bn_y1[:], bn_s[:, 0, :], bn[:, 2, :], ALU.mult))
            nc.vector.tensor_tensor(bn_s[:, 1, :], bn[:, 1, :], bn_y1[:], ALU.subtract).then_inc(bn_ok, 1)
            for t in range(NT):
                dve.wait_ge(pn_mm, t + 1)
                nc.vector.tensor_tensor(agg[:, t, :], bank[4 + t], b1, ALU.add).then_inc(pn_ok, 1)
            dve.wait_ge(bnr_mm, 2)
            for e in range(2):
                ins = nc.vector.tensor_copy(bn_rows[:, e, :], bank[(7, 0)[e]])
            ins.then_inc(bn_ok, 1)
            dve.wait_ge(ld_b3, 16)
            dve.wait_ge(ld_l3, 96)
            link(nc.vector.tensor_tensor(b_hh[:, 0:2 * F], b_hh[:, 0:2 * F], b_ih[:, 0:2 * F], ALU.add))
            for n in range(NT * 3):
                t, gate_ = divmod(n, 3)
                dve.wait_ge(gh_mm, n + 1)
                nc.vector.tensor_tensor(gh[:, t, gate_ * F:(gate_ + 1) * F], bank[GB[n]],
                                        b_hh[:, gate_ * F:(gate_ + 1) * F], ALU.add).then_inc(gh_ok, 1)
            for t in range(NT):
                ins = nc.vector.tensor_tensor(x[:, t, :], x[:, t, :], h[:, t, :], ALU.add)
            link(ins)
            for t in range(NT):
                ins = nc.vector.tensor_tensor(x[:, t, :], x[:, t, :], bn_rows[:, 1, :], ALU.add)
            link(ins)

            def lower(i, q):
                dve.wait_ge(hi_ok, i * LB + (q + 1))
                nc.vector.scalar_tensor_tensor(out=m_lo[:, q % 3, :], in0=got[:, q % LB, :], scalar=0.0,
                                               in1=m_hi[:, q % 3, :].bitcast(F32), op0=ALU.max,
                                               op1=ALU.subtract).then_inc(lo_ok, 1)

            def messages(i, first):
                for q in range(LB):
                    dve.wait_ge(ld_got[q], i * 16 + 16)
                    dve.wait_ge(pre_mm, i * LB + (q + 1))
                    nc.vector.tensor_tensor(got[:, q, :], got[:, q, :], bank[3 + q % 3], ALU.add).then_inc(sum_ok, 1)
                    if not (first and q < 3):
                        dve.wait_ge(scat, i * LB + (q - 2))
                    nc.vector.tensor_scalar(oh_r[:, q % 3, :], iota32[:], dst_f[:, bass.ds(i * LB + q, 1)], None,
                                            ALU.is_equal)
                    if not (first and q < 1):
                        lower(i, q - 1)

            messages(0, True)
            with dve.Fori(1, ET // LB) as i:
                messages(i, False)
            lower(ET // LB - 1, LB - 1)
            dve.wait_ge(scat, ET)
            for t in range(NT):
                nc.vector.tensor_copy(agg[:, t, :], bank[t]).then_inc(agg_v, 1)
            for c in range(FC):
                dve.wait_ge(aggT_mm, c + 1)
                nc.vector.tensor_copy(aggT[:, c, :], bank[3 + c][:, 0:N]).then_inc(aggT_ok, 1)
            for c in range(FC):
                dve.wait_ge(mT_mm, c + 1)
                nc.vector.scalar_tensor_tensor(out=mT[:, c, :], in0=deg_row[:], scalar=bn[:, 4, c:c + 1],
                                               in1=bank[(7, 0, 1, 2)[c]][:, 0:N], op0=ALU.mult,
                                               op1=ALU.add).then_inc(mT_ok, 1)
            for t in range(NT):
                b = [(3 + 3 * t + e) % 8 for e in range(3)]
                rz, n_, d_ = grz[:, t % 2], gn[:, t % 2], gd[:, t % 2]
                dve.wait_ge(gi_mm, 3 * t + 2)
                nc.vector.tensor_tensor(rz[:, 0:F], bank[b[0]], gh[:, t, 0:F], ALU.add)
                nc.vector.tensor_tensor(rz[:, F:2 * F], bank[b[1]], gh[:, t, F:2 * F], ALU.add).then_inc(gs_v, 1)
                dve.wait_ge(gi_mm, 3 * t + 3)
                nc.vector.tensor_tensor(n_, bank[b[2]], b_ih[:, 2 * F:3 * F], ALU.add)
                dve.wait_ge(gs_s, t + 1)
                link(nc.vector.tensor_tensor(d_, rz[:, 0:F], gh[:, t, 2 * F:3 * F], ALU.mult))
                nc.vector.tensor_tensor(n_, n_, d_, ALU.add).then_inc(gn_v, 1)
                dve.wait_ge(gn_s, t + 1)
                link(nc.vector.tensor_tensor(d_, h[:, t, :], n_, ALU.subtract))
                link(nc.vector.tensor_tensor(d_, d_, rz[:, F:2 * F], ALU.mult))
                link(nc.vector.tensor_tensor(d_, d_, n_, ALU.add))
                link(nc.vector.tensor_tensor(d_, d_, bn_rows[:, 0, :], ALU.mult))
                nc.vector.tensor_tensor(x[:, t, :], x[:, t, :], d_, ALU.add).then_inc(out_ok, 1)

        @block.tensor
        def _(pe):
            def chain(o, pairs, first=True, last=True):
                for n, (l, r) in enumerate(pairs):
                    ins = nc.tensor.matmul(o, l, r, start=first and n == 0, stop=last and n == len(pairs) - 1)
                return ins

            def transpose_h():
                for c in range(FC):
                    for t in range(NT):
                        ins = nc.tensor.transpose(bank[c][:, cols(t)], h[:, t, cols(c)], ident[:])
                    ins.then_inc(hT_mm, 1)

            def attention_vectors():
                pe.wait_ge(ld_gab, 64)
                pe.wait_ge(ld_gaT[0], 16)
                v = bank[0][:, 0:FC * 16].rearrange("p (c e n) -> p c e n", c=FC, e=2)
                for c in range(FC):
                    for hd in range(HEADS):
                        ins = nc.tensor.matmul(v[:, c, :, hd], ga_wT[0][:, hd, cols(c)], ga_a[0][:, hd, :],
                                               start=True, stop=True)
                ins.then_inc(wa_mm, 1)
                pe.wait_ge(ld_gaT[1], 16)
                v = bank[1][:, 0:2 * FC * 16].rearrange("p (c e n) -> p c e n", c=2 * FC, e=2)
                for c in range(2 * FC):
                    for j in range(FC):
                        ins = nc.tensor.matmul(v[:, c, :, 2 * j:2 * j + 2].rearrange("p s e -> p e s"),
                                               ga_wT[1][:, j, cols(c)], ga_a[1][:, :, j, :], start=True, stop=True)
                ins.then_inc(wa_mm, 1)

            def relational(l, s):
                pe.wait_ge(hT_v, 2 + FC * s)
                pe.wait_ge(ld_l1, 32)
                for t in range(NT):
                    ins = chain(bank3(4, REL)[:, t, :], [(hT[:, c, cols(t)], gw[:, l, c, :]) for c in range(FC)])
                ins.then_inc(gate_mm, 1)
                pe.wait_ge(gx_ok, REL * NT * (l + 1))
                for g in range(REL * FC):
                    r, c = divmod(g, FC)
                    cT = (c0T, c1T)[r]
                    chain(bank[YB[g]][:, 0:N], [(gx[:, r, j, cols(c)], cT[:, j, :]) for j in range(NT)]
                          ).then_inc(yT_mm, 1)
                pe.wait_ge(yT_v, REL * FC * (l + 1))
                for t in range(NT):
                    chain(bank[5 + t], [(hT[:, c, cols(t)], roots[:, l, c, :]) for c in range(FC)], last=False)
                pe.wait_ge(w_ok, 4 * (l + 1))
                for t in range(NT):
                    chain(bank[5 + t], [(yT[:, g, cols(t)], w_mix[l][:, g * F:(g + 1) * F])
                                        for g in range(REL * FC)], first=False).then_inc(rg_mm, 1)

            pe.wait_ge(ident_ok, 1)
            pe.wait_ge(h_ok, NT)
            transpose_h()
            pe.wait_ge(hT_v, 2)
            pe.wait_ge(hT_s, 2)
            pe.wait_ge(ld_l0, 64)
            chain(bank[4][0:D0, 0:N], [(wqk[:, c, 0:D0], hT[:, c, :]) for c in range(FC)]).then_inc(l0_mm, 1)
            chain(bank[5][0:D0, 0:N], [(wqk[:, c, D0:2 * D0], hT[:, c, :]) for c in range(FC)]
                  ).then_inc(l0_mm, 1)
            for t in range(NT):
                ins = chain(bank3(6, D0)[:, t, :], [(hT[:, c, cols(t)], wv[:, c, F - D0:F]) for c in range(FC)])
            ins.then_inc(l0_mm, 1)
            pe.wait_ge(hsum_ok, 1)
            chain(bank[7][:, 0:F - D0], [(hsum[:, c:c + 1].to_broadcast([P, P]), wv[:, c, 0:F - D0])
                                         for c in range(FC)]).then_inc(l0_mm, 1)

            def count(i, first, last, tiles=CB):
                for q in range(tiles):
                    k = q % EB
                    pe.wait_ge(oh_ok, i * CB + (q + 1))
                    for j in range(NT):
                        for b, lo in ((j, 0), (3 + j, N)):
                            ins = nc.tensor.matmul(bank[b][:, 0:N], oh_d[:, k, cols(j)], oh_s[:, k, lo:lo + N],
                                                   start=first and q == 0, stop=last and q == tiles - 1)
                    ins.then_inc(oh_used, 1)

            pe.wait_ge(qk_ok, 2)
            count(0, True, False)
            with pe.Fori(1, CT - 1) as i:
                count(i, False, False)
            count(CT - 1, False, True, ET - CB * (CT - 1))
            pe.wait_ge(cnt_ok, NT)
            for t in range(NT):
                for j in range(NT):
                    ins = nc.tensor.transpose(bank[t][:, cols(j)], cntT[:, j, cols(t)], ident[:])
                ins.then_inc(cntn_mm, 1)
            pe.wait_ge(cnt_ok, 2 * NT)
            for t in range(NT):
                nc.tensor.matmul(bank[3 + t][:, 0:N], qT[:, cols(t)], kT, start=True, stop=True).then_inc(sc_mm, 1)
            pe.wait_ge(cntn_ok, NT)
            pe.wait_ge(v_ok, 1)
            chain(bank[6][:, 0:N], [(ones[:], cnt[:, t, :]) for t in range(NT)]).then_inc(deg_mm, 1)
            pe.wait_ge(ex_ok, NT)
            for j in range(NT):
                for t in range(NT):
                    ins = nc.tensor.transpose(bank[j][:, cols(t)], att[:, t, cols(j)], ident[:])
                ins.then_inc(attT_mm, 1)
            pe.wait_ge(attT_ok, NT)
            for t in range(NT):
                ins = chain(bank3(7, D0)[:, t, :], [(attT[:, j, cols(t)], v7[:, j, :]) for j in range(NT)])
            ins.then_inc(o7_mm, 1)

            pe.wait_ge(h_ok, 2 * NT)
            transpose_h()
            relational(0, 1)
            pe.wait_ge(h2_ok, NT)
            transpose_h()
            relational(1, 2)

            def attention(g):
                nh, kc, inT = C[g], FC * (g + 1), (oT if g else hT)
                done = g * HEADS
                pe.wait_ge(wa_ok, g + 1)
                chain(bank[4][0:40, 0:N], [(wa[g][:, c, :], inT[:, c, :]) for c in range(kc)]).then_inc(aT_mm, 1)
                pe.wait_ge(aT_ok, g + 1)
                for t in range(NT):
                    ins = nc.tensor.transpose(bank3(5, 40)[:, t, :], aT[:, cols(t)], ident[0:40, 0:40])
                ins.then_inc(ac_mm, 1)
                pe.wait_ge(ld_ga[g], 16)
                banks, per = hx_banks(g)
                for hd in range(HEADS):
                    if hd == 1:
                        pe.wait_ge(ac_ok, g + 1)
                    if hd >= 2:
                        pe.wait_ge(far_ok, done + hd - 1)
                    nc.tensor.matmul(bank[4 + hd % 2][:, 0:N], ident[0:HEADS, hd:hd + 1].to_broadcast([HEADS, P]),
                                     aT[0:HEADS, :], start=True, stop=True).then_inc(as_mm, 1)
                    if hd < len(banks):
                        t, part = divmod(hd, per)
                        chain(bank[banks[hd]], [(inT[:, c, cols(t)], ga_w[g][:, c, part * F:(part + 1) * F])
                                                for c in range(kc)]).then_inc(hx_mm, 1)
                pe.wait_ge(rc_ok, g + 1)
                for t in range(NT):
                    ins = nc.tensor.transpose(bank[4][0:40, cols(t)], rcols[:, t, :], ident[:])
                ins.then_inc(rT_mm, 1)
                pe.wait_ge(rT_ok, g + 1)
                pe.wait_ge(hx_ok, 2 * NT + g * NT)

                def row_terms(hd):
                    n = done + hd
                    if hd >= 2:
                        pe.wait_ge(lr_ok, n - 1)
                    for e in range(2):
                        nc.tensor.matmul(bank[4 + 2 * e + hd % 2][:, 0:N],
                                         ident[32 * e:32 * e + HEADS, 32 * e + hd:32 * e + hd + 1]
                                         .to_broadcast([HEADS, P]),
                                         rT[32 * e:32 * e + HEADS, :], start=True, stop=True).then_inc(rb_mm, 1)

                row_terms(0)
                row_terms(1)
                for hd in range(HEADS):
                    n = done + hd
                    if hd + 2 < HEADS:
                        row_terms(hd + 2)
                    pe.wait_ge(pg_ok, n + 1)
                    if n >= 2:
                        pe.wait_ge(pv_used, n - 1)
                    o = bank3(hd % 2, nh + 1)
                    for j in range(NT):
                        ins = chain(o[:, j, :], [(ex[:, hd % 3, t, cols(j)], hx[g][:, t, hd, :])
                                                 for t in range(NT)])
                    ins.then_inc(pv_mm, 1)

            attention_vectors()
            pe.wait_ge(wa_ok, 2)
            pe.wait_ge(h_ok, 3 * NT)
            transpose_h()
            pe.wait_ge(hT_v, 2 * 2 + FC * 2)
            pe.wait_ge(hT_s, 2 * 2)
            attention(0)
            pe.wait_ge(pv_used, HEADS)
            for c in range(2 * FC):
                for t in range(NT):
                    ins = nc.tensor.transpose(bank[c][:, cols(t)], o_ga[0][:, t, cols(c)], ident[:])
                ins.then_inc(oT_mm, 1)
            pe.wait_ge(oT_v, FC)
            pe.wait_ge(oT_s, FC)
            pe.wait_ge(set_ok, 2)
            attention(1)

            pe.wait_ge(h_ok, 4 * NT)
            transpose_h()
            pe.wait_ge(hT_v, 2 * 3 + FC * 2)
            pe.wait_ge(hT_s, 2 * 3)
            pe.wait_ge(ld_l3, 96)
            for t in range(NT):
                chain(bank[4 + t], [(hT[:, c, cols(t)], w1a[:, c, :]) for c in range(FC)]).then_inc(pn_mm, 1)
            pe.wait_ge(bn_ok, 1)
            for e in range(2):
                for c in range(FC):
                    ins = nc.tensor.matmul(bank[(7, 0)[e]][:, cols(c)], bn_s[:, e, c:c + 1].to_broadcast([P, P]),
                                           ident[:], start=True, stop=True)
                ins.then_inc(bnr_mm, 1)
            for n in range(NT * 3):
                t, gate_ = divmod(n, 3)
                if n >= 3:
                    pe.wait_ge(gh_ok, n - 2)
                chain(bank[GB[n]], [(hT[:, c, cols(t)], w_hh[:, c, gate_ * F:(gate_ + 1) * F])
                                    for c in range(FC)]).then_inc(gh_mm, 1)
            pe.wait_ge(gh_ok, 9)
            pe.wait_ge(bn_ok, 2)

            def edge_part(i, q, first):
                if q % LC == 0:
                    pe.wait_ge(ld_ea[q // LC], i * 32 + 32)
                if not (first and q < 3):
                    pe.wait_ge(sum_ok, i * LB + (q - 2))
                nc.tensor.matmul(bank[3 + q % 3], ea[:, q // LC, cols(q % LC)], w1b[:], start=True, stop=True
                                 ).then_inc(pre_mm, 1)

            def scatter(i, q, first=False, last=False):
                pe.wait_ge(lo_ok, i * LB + (q + 1))
                for j in range(NT):
                    for m in (m_hi, m_lo):
                        ins = nc.tensor.matmul(bank[j], oh_r[:, q % 3, cols(j)], m[:, q % 3, :],
                                               start=first and m is m_hi, stop=last and m is m_lo)
                ins.then_inc(scat, 1)

            for q in range(LB):
                edge_part(0, q, True)
                if q >= 2:
                    scatter(0, q - 2, first=q == 2)
            with pe.Fori(1, ET // LB) as i:
                for q in range(LB):
                    edge_part(i, q, False)
                    scatter(i, q - 2)
            for q in (LB - 2, LB - 1):
                scatter(ET // LB - 1, q, last=q == LB - 1)
            pe.wait_ge(agg_v, NT)
            for c in range(FC):
                for t in range(NT):
                    ins = nc.tensor.transpose(bank[3 + c][:, cols(t)], agg[:, t, cols(c)], ident[:])
                ins.then_inc(aggT_mm, 1)
            pe.wait_ge(aggT_ok, FC)
            pe.wait_ge(ld_ih, 32)
            for c in range(FC):
                chain(bank[(7, 0, 1, 2)[c]][:, 0:N], [(w2[:, k, cols(c)], aggT[:, k, :]) for k in range(FC)]
                      ).then_inc(mT_mm, 1)
            pe.wait_ge(mT_ok, FC)
            for t in range(NT):
                for e in range(3):
                    if t == 2 and e == 2:
                        pe.wait_ge(gs_v, 1)
                    chain(bank[(3 + 3 * t + e) % 8], [(mT[:, c, cols(t)], w_ih[:, c, e * F:(e + 1) * F])
                                                      for c in range(FC)]).then_inc(gi_mm, 1)


def kernel(**inputs):
    import numpy as np
    import concourse.bacc as bacc
    from concourse.bass_utils import run_bass_kernel_spmd

    def get(name):
        return np.asarray(inputs[name])

    def chunks(w):
        return w.reshape(-1, P, w.shape[1]).transpose(1, 0, 2)

    def halves(basis):
        return basis.reshape(-1, 2, 2, P, F).transpose(3, 0, 1, 2, 4).reshape(P, -1, HALF)

    basis = [get("L1_gnn_basis1"), get("L1_gnn_basis2")]
    lay = {
        "x": chunks(get("x")),
        "edge": np.stack([get(n).reshape(ET, P).T for n in ("src", "dst", "edge_type_2")], axis=1),
        "wqk": chunks(np.concatenate([get("L0_gnn_Wq")[:, F - D0:], get("L0_gnn_Wk")[:, F - D0:]], axis=1)),
        "bqk": np.stack([get("L0_gnn_bq")[F - D0:], get("L0_gnn_bk")[F - D0:]], axis=1),
        "wv": chunks(get("L0_gnn_Wv")),
        "rows": np.stack([get("L0_gnn_bv"), get("L1_gnn_bias1"), get("L1_gnn_bias2")]),
        "mixc": np.stack([get("L1_gnn_att1").T, get("L1_gnn_att2").T]),
        "gw": np.stack([get(f"L1_gnn_gate_w{l}")[:, :, 0].reshape(REL, FC, P).transpose(2, 1, 0) for l in (1, 2)], axis=1),
        "roots": np.stack([chunks(get("L1_gnn_root1")), chunks(get("L1_gnn_root2"))], axis=1),
        "basis_v": np.concatenate([halves(b[:MIX_V]) for b in basis], axis=1),
        "basis_g": np.concatenate([halves(b[MIX_V:]) for b in basis], axis=1),
        "ga_w1": chunks(get("L2_gnn_W1")),
        "ga_w1T": chunks(get("L2_gnn_W1").T),
        "ga_w2": chunks(get("L2_gnn_W2")),
        "ga_w2T": chunks(get("L2_gnn_W2").T),
        "ga_a1": np.stack([get("L2_gnn_att_src1"), get("L2_gnn_att_dst1")]).transpose(2, 1, 0),
        "ga_a2": np.stack([get("L2_gnn_att_src2"), get("L2_gnn_att_dst2")]).reshape(2, FC, 2, C2).transpose(3, 2, 1, 0),
        "ga_b": np.concatenate([get("L2_gnn_b1"), get("L2_gnn_b2")]),
        "edge_attr": get("edge_attr_128").T.reshape(ED, ET // LC, LC * P),
        "src_idx": get("src").reshape(ET // LC, LC, P).transpose(2, 0, 1),
        "w1a": chunks(get("L3_gnn_W1").T[:F]),
        "w1b": get("L3_gnn_W1").T[F:],
        "b1": get("L3_gnn_b1"),
        "w2": chunks(get("L3_gnn_W2").T),
        "w_ih": chunks(get("L3_gnn_W_ih").T),
        "w_hh": chunks(get("L3_gnn_W_hh").T),
        "b_ih": get("L3_gnn_b_ih"),
        "b_hh": get("L3_gnn_b_hh"),
        "bn": np.stack([get(f"L3_gnn_{n}").reshape(FC, P).T for n in ("gamma", "beta", "run_mean", "run_var", "b2")], axis=1),
    }
    nc = bacc.Bacc("TRN2", target_bir_lowering=False, num_devices=1)
    arrays, aps = {}, {}
    for name, v in lay.items():
        v = np.ascontiguousarray(v)
        arrays[f"{name}_dram"] = v
        aps[name] = nc.dram_tensor(f"{name}_dram", v.shape, mybir.dt.from_np(v.dtype), kind="ExternalInput").ap()
    out = nc.dram_tensor("out_dram", (N, F), F32, kind="ExternalOutput").ap()
    build(nc, aps, out.rearrange("(t p) n -> p t n", p=P))
    r = run_bass_kernel_spmd(nc, [arrays], core_ids=[0])
    return r.results[0]["out_dram"]
```

```python
from contextlib import ExitStack

import concourse.bass as bass
import concourse.mybir as mybir
from concourse.alu_op_type import AluOpType as ALU

ACT = mybir.ActivationFunctionType
AX_X = mybir.AxisListType.X
F32 = mybir.dt.float32
F32R = mybir.dt.float32r
BF16 = mybir.dt.bfloat16
F16 = mybir.dt.float16
I32 = mybir.dt.int32

P = 128
N = 384
NT = N // P
F = 512
FC = F // P
E = 12672
ET = E // P
ED = 128
HEADS = 8
D0 = F // HEADS
BASES = 30
REL = 2
LN_EPS = 1e-5
BN_EPS = 1e-5
SLOPE = 0.2
FAR = -1e30

C1, C2 = 128, 64
MIX_V = 16
MIX_G = BASES - MIX_V
PA = (12, 13, 14, 23)
HALF = FC * F // 2
UV = 2 * MIX_V
UG = 2 * MIX_G
EB = 3
CB = 18
CT = -(-ET // CB)
LB = 9
WIN = 96
STEP = 32
PAD = 16
LAG = 3
LC = 3


def build(nc, a, out):
    with ExitStack() as ctx:
        def sb(name, shape, dt=F32):
            return ctx.enter_context(nc.sbuf_tensor(name, shape, dt))

        def sem(name):
            return ctx.enter_context(nc.semaphore(name))

        ps = ctx.enter_context(nc.psum_tensor("ps", [P, 8, 512], F32))

        mixm = sb("mixm", [P, 26624])
        ring_v = mixm[:, 0:4096].rearrange("p (k n) -> p k n", k=4)
        ring_g = mixm[:, 4096:6144].rearrange("p (k n) -> p k n", k=2)
        prod = mixm[:, 6144:10240].rearrange("p (k r n) -> p k r n", k=2, r=REL)
        acc_g = [mixm[:, o:o + 4096] for o in (10240, 18432)]
        w_mix = [mixm[:, o:o + 4096] for o in (14336, 22528)]

        def quarter(t, r, h):
            return t[:, (2 * r + h) * HALF:(2 * r + h + 1) * HALF]

        node = sb("node", [P, 10752])
        roots = node[:, 0:4096].rearrange("p (l c n) -> p l c n", l=2, c=FC)
        wv = node[:, 4096:6144].rearrange("p (c n) -> p c n", c=FC)
        wqk = node[:, 6144:6656].rearrange("p (c n) -> p c n", c=FC)
        attT = node[:, 6656:7808].rearrange("p (t n) -> p t n", t=NT)
        qT = node[0:D0, 7808:8192]
        kT = node[0:D0, 8192:8576]
        yT = node[:, 4096:7168].rearrange("p (g n) -> p g n", g=REL * FC)
        gx = node[:, 7168:10240].rearrange("p (r t n) -> p r t n", r=REL, t=NT)
        oh = node[:, 8576:10304].bitcast(BF16)
        oh_s = oh[:, 0:EB * N].rearrange("p (k n) -> p k n", k=EB)
        oh_d = oh[:, EB * N:EB * 3 * N].rearrange("p (k e n) -> p k e n", k=EB, e=2)

        x = sb("x", [P, NT, F])
        h = sb("h", [P, NT, F])
        hT = sb("hT", [P, FC, N])
        att = h[:, :, 0:N]
        rows = sb("rows", [P, 3, F])
        deg_row = sb("deg_row", [P, N])

        iota32 = sb("iota32", [P, N])
        pidx = sb("pidx", [P, 1])
        ident = sb("ident", [P, P])
        ones = sb("ones", [P, P])
        dst_f = sb("dst_f", [P, ET])
        dstw_f = sb("dstw_f", [P, ET])
        outside = sb("outside", [P, 1])
        outside_i = sb("outside_i", [P, 1], I32)
        zero = sb("zero", [P, 2], BF16)
        mixc = sb("mixc", [P, 2, BASES, REL])
        gw = sb("gw", [P, 2, FC, REL])
        bqk = sb("bqk", [D0, 2])
        stats = sb("stats", [P, NT, 6])
        mv = sb("mv", [P, NT, 2])
        ve = sb("ve", [P, NT])
        lnv = sb("lnv", [P, NT])
        y0 = sb("y0", [P, NT])
        y1 = sb("y1", [P, NT])
        rstd = sb("rstd", [P, NT])
        nbias = sb("nbias", [P, NT])
        hsum = sb("hsum", [P, FC])
        smax = sb("smax", [P, NT])
        ssum = sb("ssum", [P, NT])
        srec = sb("srec", [P, NT])
        gate = sb("gate", [P, NT, REL])

        W1O, W2O = 18432, 10240
        ga_w = [mixm[:, 10240:14336].rearrange("p (c n) -> p c n", c=FC),
                mixm[:, 0:4096].rearrange("p (c n) -> p c n", c=2 * FC)]
        ga_wT = [mixm[:, 14336:18432].rearrange("p (j n) -> p j n", j=HEADS),
                 mixm[:, 4096:8192].rearrange("p (j n) -> p j n", j=FC)]
        ga_b = mixm[:, 8192:9728]
        C = [C1, C2]
        hx = [node[:, 0:NT * HEADS * (c + 1)].rearrange("p (t h n) -> p t h n", t=NT, h=HEADS) for c in C]
        o_ga = [node[:, 3096:6168].rearrange("p (t n) -> p t n", t=NT),
                node[:, 1560:3096].rearrange("p (t n) -> p t n", t=NT)]
        oT = node[:, 6168:9240].rearrange("p (c n) -> p c n", c=2 * FC)
        far = node[:, 9240:10392].rearrange("p (t n) -> p t n", t=NT)
        wa = [sb("wa0", [P, FC, 40]), sb("wa1", [P, 2 * FC, 40])]
        ga_a = [sb("ga_a0", [P, HEADS, 2]), sb("ga_a1", [P, 2, FC, 2])]
        aT = mixm[0:40, 4096:4480]
        pick = sb("pick", [48, HEADS], F32R)
        pick2 = sb("pick2", [48, 2, HEADS])
        acols = sb("acols", [P, NT, 40])
        rfull = sb("rfull", [P, NT, 2, HEADS])
        rcols = sb("rcols", [P, NT, 2, 32], F32R)
        far_max = sb("far_max", [P, NT, HEADS])
        far_m = sb("far_m", [P, NT, HEADS])
        as02 = sb("as02", [P, NT, HEADS])
        den = sb("den", [P, 2, NT])
        rec = sb("rec", [P, 2, NT])
        lsum = sb("lsum", [P, NT])
        lmax = sb("lmax", [P, NT])

        w_hh = mixm[:, 18432:24576].rearrange("p (c n) -> p c n", c=FC)
        w1a = mixm[:, 24576:26624].rearrange("p (c n) -> p c n", c=FC)
        w_ih = mixm[:, 10240:16384].rearrange("p (c n) -> p c n", c=FC)
        w2 = mixm[:, 16384:18432].rearrange("p (c n) -> p c n", c=FC)
        w1b = sb("w1b", [P, F])
        b_hh = rows[:].rearrange("p a n -> p (a n)")
        b_ih = mixm[:, 8192:9728]
        b1 = mixm[:, 9728:10240]
        agg = mixm[:, 0:1536].rearrange("p (t n) -> p t n", t=NT)
        aggT = mixm[:, 1536:3072].rearrange("p (c n) -> p c n", c=FC)
        mT = mixm[:, 4096:5632].rearrange("p (c n) -> p c n", c=FC)
        bn_rows = mixm[:, 5632:6656].rearrange("p (a n) -> p a n", a=2)
        gh = node[:, 0:4608].rearrange("p (t n) -> p t n", t=NT)
        got = node[:, 4608:9216].rearrange("p (q n) -> p q n", q=LB)
        ea = node[:, 9216:10368].rearrange("p (m n) -> p m n", m=LB // LC)
        tmp = node[:, 4608:9216].rearrange("p (q n) -> p q n", q=LB)
        idx = sb("idx", [P, LB // LC, LC], I32)
        pool_mark = sb("pool_mark", [P, 1])
        bn = sb("bn", [P, 5, FC])
        bn_ve = sb("bn_ve", [P, FC])
        bn_y0 = sb("bn_y0", [P, FC])
        bn_y1 = sb("bn_y1", [P, FC])
        bn_s = sb("bn_s", [P, 2, FC])
        with nc.sbuf_tensor("early", [P, 1216], F32) as early:
            src_f, dst0_f, dst0w_f, typ0 = (early[:, ET * n:ET * (n + 1)] for n in range(4))
            start_f = early[:, 4 * ET:5 * ET]
            edge_i = early[:, 5 * ET:8 * ET].bitcast(I32).rearrange("p (e n) -> p e n", e=3)
            iota16 = early[:, 8 * ET:8 * ET + N // 2].bitcast(F16)
            v7 = early[:, 1024:1216].rearrange("p (t n) -> p t n", t=NT)
        aT_hi = sb("aT_hi", [HEADS, N], F32R)
        aT_lo = sb("aT_lo", [HEADS, N], F32R)
        rT = sb("rT", [48, N], F32R)
        rest = sb("rest", [P, 64])
        with nc.sbuf_tensor("mats", [P, 4, NT, N], F32) as mats:
            cnt, cntT, c0T, c1T = (mats[:, i] for i in range(4))
        m_hi = sb("m_hi", [P, 3, F], F32R)
        m_lo = sb("m_lo", [P, 3, F], F32R)
        oh_r = sb("oh_r", [P, 3, N], F32R)
        c0n, c1n = cntT, node[:, 8576:9728].rearrange("p (t n) -> p t n", t=NT)
        ex = mats[:, 1:4]
        zs = mixm[0:WIN, 3072:3584]
        nodes_dram = nc.dram_tensor("nodes_scratch", (N, F), F32, kind="Internal").ap()

        ld_x, ld_edge, ld_l0, ld_mixc, ld_l1 = (sem(f"ld_{n}") for n in ("x", "edge", "l0", "mixc", "l1"))
        ld_v = [sem(f"ld_v{k}") for k in range(4)]
        ld_g = [sem(f"ld_g{k}") for k in range(2)]
        out_sem = sem("out_sem")
        consts = sem("consts")
        out_cnt = sem("out_cnt")
        out_mm = sem("out_mm")
        out_set = sem("out_set")
        sums_ok = sem("sums_ok")
        ident_ok = sem("ident_ok")
        v_step = sem("v_step")
        s_step = sem("s_step")
        ln_var = sem("ln_var")
        ln_y = sem("ln_y")
        ln_scale = sem("ln_scale")
        h_ok = sem("h_ok")
        hT_mm = sem("hT_mm")
        hT_v = sem("hT_v")
        hT_s = sem("hT_s")
        hsum_ok = sem("hsum_ok")
        l0_mm = sem("l0_mm")
        qk_ok = sem("qk_ok")
        v_ok = sem("v_ok")
        oh_ok = sem("oh_ok")
        oh_used = sem("oh_used")
        cntn_ok = sem("cntn_ok")
        cnt_ok = sem("cnt_ok")
        cntn_mm = sem("cntn_mm")
        cntT_ok = sem("cntT_ok")
        deg_mm = sem("deg_mm")
        deg_ok = sem("deg_ok")
        sc_mm = sem("sc_mm")
        sc_ok = sem("sc_ok")
        ex_ok = sem("ex_ok")
        attT_mm = sem("attT_mm")
        attT_ok = sem("attT_ok")
        o7_mm = sem("o7_mm")
        gate_mm = sem("gate_mm")
        gate_ok = sem("gate_ok")
        gx_ok = sem("gx_ok")
        yT_mm = sem("yT_mm")
        yT_v = sem("yT_v")
        w_ok = sem("w_ok")
        rg_mm = sem("rg_mm")
        h2_ok = sem("h2_ok")
        mix_done = sem("mix_done")
        prod_ok = sem("prod_ok")
        prod_added = sem("prod_added")
        x2_ok = sem("x2_ok")
        ld_ga = [sem("ld_ga0"), sem("ld_ga1")]
        ld_gaT = [sem("ld_gaT0"), sem("ld_gaT1")]
        ld_gaa = sem("ld_gaa")
        ld_gab = sem("ld_gab")
        ld_l3 = sem("ld_l3")
        ld_ih = sem("ld_ih")
        ld_b3 = sem("ld_b3")
        ld_ea = [sem(f"ld_ea{m}") for m in range(LB // LC)]
        ld_got = [sem(f"ld_got{q}") for q in range(LB)]
        set_ok = sem("set_ok")
        wa_mm = sem("wa_mm")
        wa_ok = sem("wa_ok")
        aT_mm = sem("aT_mm")
        aT_ok = sem("aT_ok")
        aT_lo_ok = sem("aT_lo_ok")
        ac_mm = sem("ac_mm")
        ac_ok = sem("ac_ok")
        as_mm = sem("as_mm")
        far_ok = sem("far_ok")
        hx_mm = sem("hx_mm")
        hx_ok = sem("hx_ok")
        rc_ok = sem("rc_ok")
        rT_mm = sem("rT_mm")
        rT_ok = sem("rT_ok")
        rb_mm = sem("rb_mm")
        low_ok = sem("low_ok")
        lr_ok = sem("lr_ok")
        exg_ok = sem("exg_ok")
        pg_ok = sem("pg_ok")
        pv_mm = sem("pv_mm")
        pv_used = sem("pv_used")
        oT_mm = sem("oT_mm")
        oT_v = sem("oT_v")
        oT_s = sem("oT_s")
        ls_max = sem("ls_max")
        ls_sum = sem("ls_sum")
        bn_var = sem("bn_var")
        bn_y = sem("bn_y")
        bn_ok = sem("bn_ok")
        bnr_mm = sem("bnr_mm")
        pn_mm = sem("pn_mm")
        pn_ok = sem("pn_ok")
        pn_st = sem("pn_st")
        gh_mm = sem("gh_mm")
        gh_ok = sem("gh_ok")
        marks = sem("marks")
        pre_mm = sem("pre_mm")
        sum_ok = sem("sum_ok")
        hi_ok = sem("hi_ok")
        lo_ok = sem("lo_ok")
        z_ok = sem("z_ok")
        z_used = sem("z_used")
        scat = sem("scat")
        agg_v = sem("agg_v")
        aggT_mm = sem("aggT_mm")
        aggT_ok = sem("aggT_ok")
        mT_mm = sem("mT_mm")
        mT_ok = sem("mT_ok")
        gi_mm = sem("gi_mm")
        gs_v = sem("gs_v")
        gs_s = sem("gs_s")
        gn_v = sem("gn_v")
        gn_s = sem("gn_s")
        out_ok = sem("out_ok")

        bank = [ps[:, b, :] for b in range(8)]

        def bank3(b, w):
            return bank[b][:, 0:NT * w].rearrange("p (t n) -> p t n", t=NT)

        def cols(t):
            return slice(t * P, (t + 1) * P)

        def load_mix_v(eng, u, k):
            eng.dma_start(ring_v[:, k:k + 1, :], a["basis_v"][:, bass.ds(u, 1), :]).then_inc(ld_v[k], 16)

        def load_mix_g(eng, u, k):
            eng.dma_start(ring_g[:, k:k + 1, :], a["basis_g"][:, bass.ds(u, 1), :]).then_inc(ld_g[k], 16)

        CB_T = [0, 1, 2, 0, 1, 2]
        YB = [5, 6, 7, 0, 1, 2, 3, 4]

        def hx_banks(g):
            return ([0, 1, 2], 1) if g else ([0, 1, 2, 3, 6, 7], 2)

        grz = tmp[:, 0:4, :].rearrange("p (b a) n -> p b (a n)", b=2)
        gn = tmp[:, 4:6, :]
        gd = tmp[:, 6:8, :]
        GB = [1, 2, 3, 1, 2, 3, 1, 2, 3]

        block = ctx.enter_context(nc.Block())

        @block.sync
        def _(sp):
            sp.dma_start(x[:], a["x"]).then_inc(ld_x, 16)
            sp.dma_start(edge_i[:], a["edge"]).then_inc(ld_edge, 16)
            sp.dma_start(wqk, a["wqk"]).then_inc(ld_l0, 16)
            sp.dma_start(bqk[:], a["bqk"]).then_inc(ld_l0, 16)
            sp.dma_start(wv, a["wv"]).then_inc(ld_l0, 16)
            sp.dma_start(rows[:], a["rows"].partition_broadcast(P)).then_inc(ld_l0, 16)
            sp.dma_start(mixc[:], a["mixc"].partition_broadcast(P)).then_inc(ld_mixc, 16)
            for k in range(2):
                load_mix_v(sp, k, k)
            sp.dma_start(ga_a[0][:], a["ga_a1"]).then_inc(ld_gaa, 16)
            sp.wait_ge(set_ok, 1)
            for e in range(2):
                sp.dma_start(ga_a[1][e * C2:(e + 1) * C2, e], a["ga_a2"][:, e]).then_inc(ld_gaa, 16)
            sp.dma_start(gw[:], a["gw"]).then_inc(ld_l1, 16)
            sp.dma_start(roots, a["roots"]).then_inc(ld_l1, 16)

            with sp.Fori(1, CT) as i:
                for k in range(2):
                    sp.wait_ge(mix_done, i * 4 + (2 * k - 2))
                    load_mix_v(sp, i * 2 + k, k)

            def mix_loads(i0, i1):
                with sp.Fori(i0, i1) as i:
                    for k in range(4):
                        sp.wait_ge(mix_done, i * 8 + (2 * k - 6))
                        load_mix_v(sp, i * 4 + k, k)

            for k in range(4):
                if k < 2:
                    sp.wait_ge(mix_done, 4 * CT + 2 * k - 2)
                load_mix_v(sp, 2 * CT + k, k)
            mix_loads(CT // 2 + 1, UV // 4 + 1)
            sp.wait_ge(w_ok, 4)
            sp.dma_start(ga_w[0], a["ga_w1"]).then_inc(ld_ga[0], 16)
            mix_loads(UV // 4 + 1, UV // 4 + 4)
            sp.wait_ge(rg_mm, NT)
            sp.dma_start(ga_wT[0], a["ga_w1T"]).then_inc(ld_gaT[0], 16)
            mix_loads(UV // 4 + 4, 2 * UV // 4)
            sp.wait_ge(mix_done, 2 * 2 * UV)
            sp.dma_start(ga_w[1], a["ga_w2"]).then_inc(ld_ga[1], 16)
            sp.wait_ge(prod_added, 2 * 4 * (MIX_G - 1))
            sp.dma_start(ga_b, a["ga_b"].partition_broadcast(P)).then_inc(ld_gab, 16)
            sp.dma_start(b1, a["b1"].partition_broadcast(P)).then_inc(ld_l3, 16)
            sp.dma_start(w1b[:], a["w1b"]).then_inc(ld_l3, 16)
            sp.dma_start(bn[:], a["bn"]).then_inc(ld_l3, 16)
            sp.wait_ge(rg_mm, 2 * NT)
            sp.dma_start(w1a, a["w1a"]).then_inc(ld_l3, 16)
            sp.dma_start(w_hh, a["w_hh"]).then_inc(ld_l3, 16)
            sp.wait_ge(x2_ok, NT)
            sp.dma_start(b_hh, a["b_hh"].partition_broadcast(P)).then_inc(ld_l3, 16)
            sp.wait_ge(hx_mm, 2 * NT)
            sp.dma_start(w_ih, a["w_ih"]).then_inc(ld_ih, 16)
            sp.dma_start(w2, a["w2"]).then_inc(ld_ih, 16)
            sp.wait_ge(pv_used, 2 * HEADS)
            sp.dma_start(b_ih, a["b_ih"].partition_broadcast(P)).then_inc(ld_b3, 16)
            sp.wait_ge(ls_sum, 1)

            def edges(i, first):
                for m in range(LB // LC):
                    if not first:
                        sp.wait_ge(sum_ok, i * LB + (LC * m - LB + LC))
                    at = bass.ds(i * (LB // LC) + m, 1)
                    sp.dma_start(ea[:, m:m + 1, :], a["edge_attr"][:, at, :]).then_inc(ld_ea[m], 16)
                    sp.dma_start(idx[:, m:m + 1, :], a["src_idx"][:, at, :]).then_inc(ld_ea[m], 16)

            edges(0, True)
            sp.wait_ge(pn_ok, NT)
            sp.dma_start(nodes_dram.rearrange("(t p) n -> p t n", p=P), agg).then_inc(pn_st, 16)
            with sp.Fori(1, ET // LB) as i:
                edges(i, False)
            for t in range(NT):
                sp.wait_ge(out_ok, t + 1)
                sp.dma_start(out[:, t, :], x[:, t, :]).then_inc(out_sem, 16)
            sp.wait_ge(out_sem, 16 * NT)

        @block.gpsimd
        def _(pool):
            nc.gpsimd.iota(iota32[:], [[1, N]], base=0, channel_multiplier=0,
                           allow_small_or_imprecise_dtypes=True)
            nc.gpsimd.iota(iota16[:], [[1, N]], base=0, channel_multiplier=0,
                           allow_small_or_imprecise_dtypes=True)
            nc.gpsimd.iota(start_f[:], [[STEP, ET // LB], [0, LB]], base=-PAD, channel_multiplier=0,
                           allow_small_or_imprecise_dtypes=True)
            nc.gpsimd.iota(pidx[:], [[0, 1]], base=0, channel_multiplier=1,
                           allow_small_or_imprecise_dtypes=True).then_inc(consts, 1)

            def add_products(layer, i):
                for k in range(2):
                    for r in range(REL):
                        pool.wait_ge(prod_ok, i * 4 + (2 * k + r + 1))
                        if not isinstance(i, int):
                            pool.wait_ge(prod_added, i * 4 + (2 * k + r - 3 - 4 * (layer + 1)))
                        acc = quarter(acc_g[layer], r, k)
                        nc.gpsimd.tensor_tensor(acc, acc, prod[:, k, r, :], ALU.add).then_inc(prod_added, 1)

            add_products(0, 1)
            with pool.Fori(2, MIX_G) as i:
                add_products(0, i)
            with pool.Fori(MIX_G + 1, 2 * MIX_G) as i:
                add_products(1, i)

            for n in range(2 * HEADS):
                pool.wait_ge(exg_ok, n + 1)
                hd = n % HEADS
                nc.gpsimd.tensor_tensor(ex[:, hd % 3], ex[:, hd % 3], cnt, ALU.mult).then_inc(pg_ok, 1)

            nc.gpsimd.memset(pool_mark[:], 0.0).then_inc(marks, 1)
            pool.wait_ge(pn_st, 16)

            def mark(n):
                pool.wait_ge(marks, n)
                nc.gpsimd.tensor_tensor(pool_mark[:], pool_mark[:], pool_mark[:], ALU.add).then_inc(marks, 1)

            def gathers(i, first):
                n = 1 if first else i * (LB + LB // LC) + (1 - LB)
                for q in range(LB):
                    if q % LC == 0:
                        pool.wait_ge(ld_ea[q // LC], i * 32 + 32)
                        mark(n)
                        n = n + 1
                    if not first:
                        pool.wait_ge(lo_ok, i * LB + (q - LB + 1))
                        mark(n)
                        n = n + 1
                    nc.gpsimd.indirect_dma_start(
                        out=got[:, q, :], out_offset=None, in_=nodes_dram,
                        in_offset=bass.IndirectOffsetOnAxis(ap=idx[:, q // LC, q % LC:q % LC + 1], axis=0)
                    ).then_inc(ld_got[q], 16)

            gathers(0, True)
            with pool.Fori(1, ET // LB) as i:
                gathers(i, False)

        @block.scalar
        def _(act):
            def ln_act(s, before=None):
                act.wait_ge(ln_var, s + 1)
                nc.scalar.activation(lnv[:], ve[:], ACT.Ln).then_inc(s_step, 1)
                act.wait_ge(s_step, (s if before is None else before) + 1)
                nc.scalar.activation(y0[:], lnv[:], ACT.Exp, scale=-0.5).then_inc(ln_y, 1)
                act.wait_ge(ln_scale, s + 1)
                for t in range(NT):
                    nc.scalar.activation(h[:, t, :], x[:, t, :], ACT.Relu, bias=nbias[:, t:t + 1],
                                         scale=rstd[:, t:t + 1]).then_inc(h_ok, 1)

            def hT_act(s):
                for c in (1, 3):
                    act.wait_ge(hT_mm, FC * s + c + 1)
                    nc.scalar.copy(hT[:, c, :], bank[c][:, 0:N]).then_inc(hT_s, 1)

            flat = mixc[:].rearrange("p l b r -> p (l b) r")

            def products(layer, i0, i1):
                base = layer * BASES + MIX_V

                def turn(i, first=False, last=False):
                    def operands(k):
                        act.wait_ge(ld_g[k], (i + 1) * 16)
                        if not first and not (isinstance(i, int) and i == 1):
                            act.wait_ge(prod_added, i * 4 + (2 * k - 6 - 4 * layer))

                    operands(0)
                    for k in range(2):
                        for r in range(REL):
                            to = quarter(acc_g[layer], r, k) if first else prod[:, k, r, :]
                            nc.scalar.activation(to, ring_g[:, k, :], ACT.Copy,
                                                 scale=flat[:, bass.ds(i + (base - layer * MIX_G), 1), r]
                                                 ).then_inc(prod_ok, 1)
                        if k == 0:
                            operands(1)
                        if not last:
                            act.wait_ge(prod_ok, i * 4 + (2 * k + 2))
                            load_mix_g(act, i * 2 + (2 + k), k)

                if i0 == 0:
                    act.wait_ge(ld_mixc, 16)
                if i0 == layer * MIX_G:
                    turn(i0, first=True)
                    i0 += 1
                if i0 == 1 < i1:
                    turn(1)
                    i0 += 1
                last = i1 == 2 * MIX_G
                if i1 - last > i0:
                    with act.Fori(i0, i1 - last) as i:
                        turn(i)
                if last:
                    turn(2 * MIX_G - 1, last=True)

            def products_from(i0, i1):
                if i0 < MIX_G:
                    products(0, i0, min(i1, MIX_G))
                if i1 > MIX_G:
                    products(1, max(i0, MIX_G), i1)

            def relational_act(l):
                act.wait_ge(gate_mm, l + 1)
                nc.scalar.activation(gate[:], bank3(4, REL), ACT.Sigmoid).then_inc(gate_ok, 1)

            ln_act(0)
            for k in range(2):
                load_mix_g(act, k, k)
            hT_act(0)
            products(0, 0, 1)
            act.wait_ge(ld_l0, 64)
            for n, (t_, b) in enumerate(((qT, 4), (kT, 5))):
                act.wait_ge(l0_mm, n + 1)
                nc.scalar.activation(t_, bank[b][0:D0, 0:N], ACT.Identity,
                                     bias=bqk[:, n:n + 1]).then_inc(qk_ok, 1)
            products(0, 1, PA[0])
            for t in range(NT):
                act.wait_ge(sc_ok, t + 1)
                nc.scalar.activation(att[:, t, :], att[:, t, :], ACT.Exp, bias=smax[:, t:t + 1],
                                     accum_out=ssum[:, t:t + 1]).then_inc(ex_ok, 1)
            products_from(PA[0], PA[1])
            ln_act(1)
            products_from(PA[1], PA[2])
            relational_act(0)
            products_from(PA[2], PA[3])
            relational_act(1)
            products_from(PA[3], 2 * MIX_G)
            act.wait_ge(prod_added, 2 * 4 * (MIX_G - 1))
            act.dma_start(ga_wT[1], a["ga_w2T"]).then_inc(ld_gaT[1], 16)
            act.wait_ge(set_ok, 1)
            for g in range(2):
                act.wait_ge(wa_mm, g + 1)
                kc = FC * (g + 1)
                v = bank[g][:, 0:kc * 16].rearrange("p (c e n) -> p c e n", c=kc, e=2)
                for e in range(2):
                    ins = nc.scalar.copy(wa[g][:, :, 32 * e:32 * e + 8], v[:, :, e, :])
                ins.then_inc(wa_ok, 1)

            def attention_act(g):
                nh = C[g]
                act.wait_ge(aT_mm, g + 1)
                nc.scalar.copy(aT, bank[4][0:40, 0:N]).then_inc(aT_ok, 1)
                nc.scalar.copy(aT_hi[:], bank[4][0:HEADS, 0:N]).then_inc(aT_ok, 1)
                banks, per = hx_banks(g)
                for n, b in enumerate(banks):
                    t, part = divmod(n, per)
                    act.wait_ge(hx_mm, (2 * NT if g else 0) + n + 1)
                    heads = HEADS // per
                    nc.scalar.copy(hx[g][:, t, part * heads:(part + 1) * heads, 0:nh],
                                   bank[b].rearrange("p (h n) -> p h n", h=heads)).then_inc(hx_ok, 1)

                def low(hd):
                    n = g * HEADS + hd
                    act.wait_ge(rb_mm, 2 * n + 2)
                    if n >= 3:
                        act.wait_ge(pv_mm, g * HEADS + max(hd - 2, 0))
                    for t in range(NT):
                        nc.scalar.activation(ex[:, hd % 3, t, :], bank[6 + hd % 2][:, 0:N], ACT.Identity,
                                             bias=as02[:, t, hd:hd + 1]).then_inc(low_ok, 1)

                low(0)
                low(1)
                for hd in range(HEADS):
                    act.wait_ge(lr_ok, g * HEADS + hd + 1)
                    nc.scalar.activation(ex[:, hd % 3], ex[:, hd % 3], ACT.Exp).then_inc(exg_ok, 1)
                    if hd + 2 < HEADS:
                        low(hd + 2)

            ln_act(2)
            hT_act(3)
            attention_act(0)
            for c in range(1, 2 * FC, 2):
                act.wait_ge(oT_mm, c + 1)
                nc.scalar.activation(oT[:, c, :], bank[c][:, 0:N], ACT.Relu).then_inc(oT_s, 1)
            attention_act(1)
            act.wait_ge(ls_max, 1)
            for t in range(NT):
                ins = nc.scalar.activation(tmp[:, t, :], o_ga[1][:, t, :], ACT.Exp, bias=lmax[:, t:t + 1],
                                           accum_out=lsum[:, t:t + 1])
            ins.then_inc(s_step, 1)
            act.wait_ge(s_step, 4)
            nc.scalar.activation(lsum[:], lsum[:], ACT.Ln).then_inc(ls_sum, 1)
            act.wait_ge(bn_var, 1)
            nc.scalar.activation(bn_y0[:], bn_ve[:], ACT.Ln).then_inc(s_step, 1)
            act.wait_ge(s_step, 5)
            nc.scalar.activation(bn_y0[:], bn_y0[:], ACT.Exp, scale=-0.5).then_inc(bn_y, 1)
            ln_act(3, 5)
            hT_act(4)

            def window_out(i):
                act.wait_ge(scat, i * LB + LB)
                if not (isinstance(i, int) and i == 0):
                    act.wait_ge(z_used, i)
                nc.scalar.copy(zs, bank[7][0:WIN, :]).then_inc(z_ok, 1)

            def upper(i, first, width):
                for q in range(LB):
                    if width == WIN and q == 2 and not first:
                        window_out(i - 1)
                    act.wait_ge(sum_ok, i * LB + (q + 1))
                    if not (first and q < 3):
                        act.wait_ge(scat, i * LB + (q - 2))
                    nc.scalar.activation(m_hi[:, q % 3, :], got[:, q, :], ACT.Relu).then_inc(hi_ok, 1)

            def all_upper(width):
                upper(0, True, width)
                upper(1, False, width)
                with act.Fori(2, ET // LB) as i:
                    upper(i, False, width)
                if width == WIN:
                    window_out(ET // LB - 1)

            strays = act.value_load(outside_i[0:1, 0:1])
            with act.If(strays > 0):
                all_upper(N)
            with act.Else():
                all_upper(WIN)
            for t in range(NT):
                act.wait_ge(gs_v, t + 1)
                nc.scalar.activation(grz[:, t % 2], grz[:, t % 2], ACT.Sigmoid).then_inc(gs_s, 1)
                act.wait_ge(gn_v, t + 1)
                nc.scalar.activation(gn[:, t % 2], gn[:, t % 2], ACT.Tanh).then_inc(gn_s, 1)

        @block.vector
        def _(dve):
            steps = [0]

            def link(ins):
                steps[0] += 1
                ins.then_inc(v_step, 1)
                dve.wait_ge(v_step, steps[0])

            def ln_vec(s, fill=0):
                for t in range(NT):
                    ins = nc.vector.bn_stats(stats[:, t, :], x[:, t, :])
                link(ins)
                for t in range(NT):
                    ins = nc.vector.bn_aggr(mv[:, t, :], stats[:, t, :])
                link(ins)
                nc.vector.tensor_scalar(ve[:], mv[:, :, 1], LN_EPS, None, ALU.add).then_inc(ln_var, 1)
                if fill:
                    mix(fill)
                dve.wait_ge(ln_y, s + 1)
                link(nc.vector.tensor_tensor(y1[:], y0[:], y0[:], ALU.mult))
                link(nc.vector.tensor_tensor(y1[:], y1[:], ve[:], ALU.mult))
                link(nc.vector.tensor_scalar(y1[:], y1[:], -0.5, 1.5, ALU.mult, ALU.add))
                link(nc.vector.tensor_tensor(rstd[:], y0[:], y1[:], ALU.mult))
                nc.vector.scalar_tensor_tensor(out=nbias[:], in0=mv[:, :, 0], scalar=-1.0, in1=rstd[:],
                                               op0=ALU.mult, op1=ALU.mult).then_inc(ln_scale, 1)

            def hT_vec(s):
                for c in (range(FC) if s in (1, 2) else (0, 2)):
                    dve.wait_ge(hT_mm, FC * s + c + 1)
                    nc.vector.tensor_copy(hT[:, c, :], bank[c][:, 0:N]).then_inc(hT_v, 1)

            flat = mixc[:].rearrange("p l b r -> p (l b) r")

            def mix_unit(layer, u, k, half, landed, first=False):
                dve.wait_ge(ld_v[k], landed)
                base = layer * (BASES - MIX_V)
                b = u // 2 if isinstance(u, int) else u[0]
                u = u if isinstance(u, int) else u[1]
                for r in range(REL):
                    acc = quarter(w_mix[layer], r, half)
                    scale = flat[:, bass.ds(b + base, 1), r]
                    if first:
                        nc.vector.tensor_scalar(acc, ring_v[:, k, :], scale, None, ALU.mult).then_inc(mix_done, 1)
                    else:
                        dve.wait_ge(mix_done, u * 2 + (r - 3))
                        nc.vector.scalar_tensor_tensor(out=acc, in0=ring_v[:, k, :], scalar=scale, in1=acc,
                                                       op0=ALU.mult, op1=ALU.add).then_inc(mix_done, 1)

            def landed(u):
                return 16 * (u // 2 + 1) if u < 2 * CT else 16 * ((CT if u % 4 < 2 else 0) + u // 4 - CT // 2 + 1)

            mixed = [2 * CT]

            def mix(n):
                u0, u1 = mixed[0], mixed[0] + n
                mixed[0] = u1
                layer = u0 // UV
                u = u0
                while u < u1:
                    if u % 4 == 0 and u1 - u >= 8 and u % UV >= 2:
                        turns = (u1 - u) // 4
                        with dve.Fori(u // 4, u // 4 + turns) as i:
                            for k in range(4):
                                mix_unit(layer, (i * 2 + k // 2, i * 4 + k), k, k % 2,
                                         i * 16 + (landed(k + 2 * CT) - 16 * (CT // 2)))
                        u += 4 * turns
                    else:
                        mix_unit(layer, u, u % 4, u % 2, landed(u), first=u % UV < 2)
                        u += 1

            def merge(layer):
                dve.wait_ge(prod_added, (layer + 1) * 4 * (MIX_G - 1))
                dve.wait_ge(mix_done, (layer + 1) * 2 * UV)
                for r in range(REL):
                    for half in range(2):
                        w = quarter(w_mix[layer], r, half)
                        nc.vector.tensor_tensor(w, w, quarter(acc_g[layer], r, half), ALU.add).then_inc(w_ok, 1)

            def relational_vec(l):
                dve.wait_ge(gate_ok, l + 1)
                for r in range(REL):
                    for t in range(NT):
                        nc.vector.tensor_scalar(gx[:, r, t, :], h[:, t, :], gate[:, t, r:r + 1], None,
                                                ALU.mult).then_inc(gx_ok, 1)
                for g in range(REL * FC):
                    if g % 2 == 0:
                        mix(1)
                    dve.wait_ge(yT_mm, REL * FC * l + g + 1)
                    nc.vector.tensor_copy(yT[:, g, :], bank[YB[g]][:, 0:N]).then_inc(yT_v, 1)

            for t_ in (wa[0][:], wa[1][:], ga_a[1][:], rcols[:].bitcast(F32)):
                ins = nc.vector.memset(t_, 0.0)
            ins.then_inc(set_ok, 1)
            dve.wait_ge(consts, 1)
            nc.vector.memset(ones[:], 1.0)
            nc.vector.tensor_scalar(ident[:], iota32[:, 0:P], pidx[:, 0:1], None,
                                    ALU.is_equal).then_inc(ident_ok, 1)
            nc.vector.memset(zero[:], 0.0)
            dve.wait_ge(ident_ok, 1)
            for e in range(2):
                ins = nc.vector.tensor_tensor(pick2[:, e, :], ident[0:48, 32 * e:32 * e + HEADS],
                                              ident[0:48, 32 * e + HEADS:32 * e + 2 * HEADS], ALU.add)
            link(ins)
            link(nc.vector.tensor_tensor(pick[:], pick2[:, 0, :], pick2[:, 1, :], ALU.add))
            dve.wait_ge(ld_edge, 16)
            nc.vector.tensor_copy(src_f[:], edge_i[:, 0, :])
            nc.vector.tensor_copy(dst_f[:], edge_i[:, 1, :])
            nc.vector.tensor_copy(typ0[:], edge_i[:, 2, :])
            link(nc.vector.memset(hsum[:], 0.0))
            link(nc.vector.tensor_scalar(typ0[:], typ0[:], 0.0, None, ALU.is_equal))
            nc.vector.scalar_tensor_tensor(out=dst0_f[:], in0=dst_f[:], scalar=1.0, in1=typ0[:],
                                           op0=ALU.add, op1=ALU.mult)
            link(nc.vector.tensor_tensor(dstw_f[:], dst_f[:], start_f[:], ALU.subtract))
            nc.vector.tensor_scalar(dst0_f[:], dst0_f[:], -1.0, None, ALU.add)
            link(nc.vector.scalar_tensor_tensor(out=dst0w_f[:], in0=dstw_f[:], scalar=1.0, in1=typ0[:],
                                                op0=ALU.add, op1=ALU.mult))
            link(nc.vector.tensor_scalar(typ0[:], dstw_f[:], 0.0, None, ALU.is_lt))
            nc.vector.tensor_scalar(dst0w_f[:], dst0w_f[:], -1.0, None, ALU.add)
            link(nc.vector.scalar_tensor_tensor(out=typ0[:], in0=dstw_f[:], scalar=float(WIN - 1), in1=typ0[:],
                                                op0=ALU.is_gt, op1=ALU.add))
            nc.vector.reduce_sum(outside[:], typ0[:], AX_X).then_inc(out_cnt, 1)
            dve.wait_ge(out_mm, 1)
            nc.vector.tensor_copy(outside_i[:], bank[7][:, 511:512]).then_inc(out_set, 1)
            dve.wait_ge(ld_x, 16)
            ln_vec(0)
            hT_vec(0)
            dve.wait_ge(hT_v, 2)
            dve.wait_ge(hT_s, 2)
            nc.vector.reduce_sum(hsum[:], hT[:], AX_X).then_inc(hsum_ok, 1)
            dve.wait_ge(ld_mixc, 16)
            for k in range(2):
                mix_unit(0, k, k, k, 16, first=True)
            dve.wait_ge(ld_l0, 64)
            dve.wait_ge(l0_mm, 3)
            for t in range(NT):
                nc.vector.tensor_tensor(v7[:, t, :], bank3(6, D0)[:, t, :], rows[:, 0, F - D0:F], ALU.add)
            dve.wait_ge(l0_mm, 4)
            mean = gx[:, 0, 0, 0:F - D0]
            link(nc.vector.scalar_tensor_tensor(out=mean, in0=bank[7][:, 0:F - D0], scalar=1.0 / N,
                                                in1=rows[:, 0, 0:F - D0], op0=ALU.mult, op1=ALU.add))
            dve.wait_ge(h_ok, NT)
            for t in range(NT):
                ins = nc.vector.tensor_tensor(x[:, t, 0:F - D0], x[:, t, 0:F - D0], mean, ALU.add)
            ins.then_inc(v_ok, 1)

            def one_hots(i, first, width, tiles=CB):
                of_all, of_0 = (dstw_f, dst0w_f) if width == WIN else (dst_f, dst0_f)
                for q in range(tiles):
                    k = q % EB
                    if not (first and q < EB):
                        dve.wait_ge(oh_used, i * CB + (q - EB + 1))
                    at = bass.ds(i * CB + q, 1)
                    nc.vector.tensor_scalar(oh_s[:, k, :], iota16[:], src_f[:, at], None, ALU.is_equal)
                    for e, d in enumerate((of_all, of_0)):
                        ins = nc.vector.tensor_scalar(oh_d[:, k, e, 0:width], iota16[:, 0:width], d[:, at], None,
                                                      ALU.is_equal)
                    ins.then_inc(oh_ok, 1)
                    if q in (tiles // 3, 2 * tiles // 3) and not first:
                        e = 0 if q == tiles // 3 else 1
                        mix_unit(0, i * 2 + e if isinstance(i, int) else (i, i * 2 + e), e, e, i * 16 + 16)

            def all_one_hots(width):
                one_hots(0, True, width)
                with dve.Fori(1, CT - 1) as i:
                    one_hots(i, False, width)
                one_hots(CT - 1, False, width, ET - CB * (CT - 1))

            dve.wait_ge(out_set, 1)
            strays = dve.value_load(outside_i[0:1, 0:1])
            with dve.If(strays > 0):
                all_one_hots(N)
            with dve.Else():
                all_one_hots(WIN)
            mix(1)
            dve.wait_ge(sums_ok, 1)
            for j in range(NT):
                nc.vector.tensor_copy(cnt[:, j, :], bank[j][:, PAD:PAD + N]).then_inc(cntn_ok, 1)
            for j in range(NT):
                nc.vector.tensor_copy(c0n[:, j, :], bank[3 + j][:, PAD:PAD + N]).then_inc(cnt_ok, 1)
            dve.wait_ge(cnt_ok, NT)
            dve.wait_ge(cntn_ok, NT)
            for t in range(NT):
                ins = nc.vector.tensor_scalar(att[:, t, :], cnt[:, t, :], 0.5, None, ALU.is_gt)
            link(ins)
            nc.vector.tensor_tensor(c1n[:], cnt[:], c0n[:], ALU.subtract).then_inc(cnt_ok, 1)
            for t in range(NT):
                dve.wait_ge(sc_mm, t + 1)
                link(nc.vector.scalar_tensor_tensor(out=att[:, t, :], in0=bank[3 + t][:, 0:N],
                                                    scalar=float(D0) ** -0.5, in1=att[:, t, :],
                                                    op0=ALU.mult, op1=ALU.mult))
                link(nc.vector.reduce_max(smax[:, t:t + 1], att[:, t, :], AX_X))
                nc.vector.tensor_scalar(smax[:, t:t + 1], smax[:, t:t + 1], -1.0, None,
                                        ALU.mult).then_inc(sc_ok, 1)
            mix(1)
            dve.wait_ge(deg_mm, 1)
            nc.vector.tensor_copy(deg_row[:], bank[6][:, 0:N]).then_inc(deg_ok, 1)
            for n in range(REL * NT):
                dve.wait_ge(cntn_mm, n + 1)
                nc.vector.tensor_copy((c0T, c1T)[n // NT][:, n % NT, :], bank[CB_T[n]][:, 0:N]).then_inc(cntT_ok, 1)
            for j in range(NT):
                dve.wait_ge(attT_mm, j + 1)
                nc.vector.tensor_copy(attT[:, j, :], bank[j][:, 0:N]).then_inc(attT_ok, 1)
            dve.wait_ge(ex_ok, NT)
            link(nc.vector.reciprocal(srec[:], ssum[:]))
            mix(1)
            dve.wait_ge(o7_mm, 1)
            for t in range(NT):
                ins = nc.vector.scalar_tensor_tensor(out=x[:, t, F - D0:F], in0=bank3(7, D0)[:, t, :],
                                                     scalar=srec[:, t:t + 1], in1=x[:, t, F - D0:F],
                                                     op0=ALU.mult, op1=ALU.add)
            link(ins)
            ln_vec(1, 1)
            mix(1)
            hT_vec(1)
            mix(2)
            relational_vec(0)
            for t in range(NT):
                nc.vector.tensor_tensor(x[:, t, :], x[:, t, :], rows[:, 2, :], ALU.add)
            mix(UV - mixed[0])
            merge(0)
            mix(6)
            for t in range(NT):
                if t == NT - 1:
                    mix(2)
                dve.wait_ge(rg_mm, t + 1)
                link(nc.vector.tensor_tensor(h[:, t, :], bank[5 + t], rows[:, 1, :], ALU.add))
                nc.vector.tensor_scalar(h[:, t, :], h[:, t, :], 0.0, None, ALU.max).then_inc(h2_ok, 1)
            hT_vec(2)
            mix(1)
            relational_vec(1)
            mix(2 * UV - mixed[0])
            merge(1)
            for t in range(NT):
                dve.wait_ge(rg_mm, NT + t + 1)
                nc.vector.tensor_tensor(x[:, t, :], x[:, t, :], bank[5 + t], ALU.add).then_inc(x2_ok, 1)

            link(nc.vector.tensor_tensor(cntT[:], c0T[:], c1T[:], ALU.add))
            for t in range(NT):
                nc.vector.tensor_tensor(cnt[:, t, cols(t)], cnt[:, t, cols(t)], ident[:], ALU.add)
                ins = nc.vector.tensor_tensor(cntT[:, t, cols(t)], cntT[:, t, cols(t)], ident[:], ALU.add)
            link(ins)
            nc.vector.tensor_scalar(far, cntT, 0.5, FAR, ALU.is_lt, ALU.mult)
            nc.vector.memset(hx[0][:, :, :, C1], 1.0)
            dve.wait_ge(x2_ok, NT)
            ln_vec(2)
            hT_vec(3)

            def attention_vec(g):
                nh = C[g]
                done = g * HEADS
                dve.wait_ge(ac_mm, g + 1)
                nc.vector.tensor_copy(acols[:], bank3(5, 40)).then_inc(ac_ok, 1)
                dve.wait_ge(aT_ok, 2 * g + 2)
                nc.vector.tensor_tensor(aT_lo[:], aT[0:HEADS, :], aT_hi[:].bitcast(F32), ALU.subtract
                                        ).then_inc(aT_lo_ok, 1)
                for hd in range(HEADS):
                    dve.wait_ge(as_mm, done + hd + 1)
                    if hd >= 3:
                        dve.wait_ge(far_ok, done + hd - 2)
                    for j in range(NT):
                        ins = nc.vector.tensor_tensor_reduce(
                            out=ex[:, hd % 3, j, :], in0=bank[4 + hd % 2][:, 0:N], in1=far[:, j, :], scale=1.0,
                            scalar=2 * FAR, op0=ALU.add, op1=ALU.max, accum_out=far_max[:, j, hd:hd + 1])
                    ins.then_inc(far_ok, 1)
                dve.wait_ge(far_ok, done + HEADS)
                dve.wait_ge(ac_ok, g + 1)
                a_s, a_d = acols[:, :, 0:HEADS], acols[:, :, 32:40]
                nc.vector.tensor_scalar(as02[:], a_s, SLOPE, None, ALU.mult)
                link(nc.vector.tensor_tensor(far_m[:], far_max[:], a_d, ALU.add))
                link(nc.vector.scalar_tensor_tensor(out=far_m[:], in0=far_m[:], scalar=SLOPE, in1=far_m[:],
                                                    op0=ALU.mult, op1=ALU.max))
                nc.vector.tensor_tensor(rfull[:, :, 0, :], a_d, far_m[:], ALU.subtract)
                link(nc.vector.scalar_tensor_tensor(out=rfull[:, :, 1, :], in0=a_d, scalar=SLOPE, in1=far_m[:],
                                                    op0=ALU.mult, op1=ALU.subtract))
                link(nc.vector.tensor_copy(rcols[:, :, :, 0:HEADS], rfull[:]))
                nc.vector.tensor_tensor(rcols[:, :, :, HEADS:2 * HEADS], rfull[:],
                                        rcols[:, :, :, 0:HEADS].bitcast(F32), ALU.subtract).then_inc(rc_ok, 1)
                dve.wait_ge(rT_mm, g + 1)
                nc.vector.tensor_copy(rT[:], bank[4][0:48, 0:N]).then_inc(rT_ok, 1)

                def leaky(hd):
                    n = done + hd
                    dve.wait_ge(rb_mm, 2 * n + 1)
                    for t in range(NT):
                        dve.wait_ge(low_ok, NT * n + t + 1)
                        ins = nc.vector.scalar_tensor_tensor(
                            out=ex[:, hd % 3, t, :], in0=bank[4 + hd % 2][:, 0:N], scalar=acols[:, t, hd:hd + 1],
                            in1=ex[:, hd % 3, t, :], op0=ALU.add, op1=ALU.max)
                    ins.then_inc(lr_ok, 1)

                def normalise(hd):
                    n = done + hd
                    dve.wait_ge(pv_mm, n + 1)
                    o = bank3(hd % 2, nh + 1)
                    link(nc.vector.tensor_scalar(den[:, hd % 2, :], o[:, :, nh], 1e-16, None, ALU.add))
                    link(nc.vector.reciprocal(rec[:, hd % 2, :], den[:, hd % 2, :]))
                    for j in range(NT):
                        ins = nc.vector.scalar_tensor_tensor(
                            out=o_ga[g][:, j, hd * nh:(hd + 1) * nh], in0=o[:, j, 0:nh],
                            scalar=rec[:, hd % 2, j:j + 1],
                            in1=ga_b[:, g * HEADS * C1 + hd * nh:g * HEADS * C1 + (hd + 1) * nh],
                            op0=ALU.mult, op1=ALU.add)
                    ins.then_inc(pv_used, 1)

                leaky(0)
                leaky(1)
                for hd in range(HEADS):
                    if hd + 2 < HEADS:
                        leaky(hd + 2)
                    normalise(hd)

            dve.wait_ge(ld_gab, 16)
            attention_vec(0)
            for c in range(0, 2 * FC, 2):
                dve.wait_ge(oT_mm, c + 1)
                nc.vector.tensor_scalar(oT[:, c, :], bank[c][:, 0:N], 0.0, None, ALU.max).then_inc(oT_v, 1)
            nc.vector.memset(hx[1][:, :, :, C2], 1.0).then_inc(set_ok, 1)
            attention_vec(1)
            dve.wait_ge(pv_used, 2 * HEADS)
            link(nc.vector.reduce_max(smax[:], o_ga[1], AX_X))
            nc.vector.tensor_scalar(lmax[:], smax[:], -1.0, None, ALU.mult).then_inc(ls_max, 1)
            dve.wait_ge(ld_l3, 96)
            nc.vector.tensor_scalar(bn_ve[:], bn[:, 3, :], BN_EPS, None, ALU.add).then_inc(bn_var, 1)
            dve.wait_ge(ls_sum, 1)
            link(nc.vector.tensor_tensor(lsum[:], smax[:], lsum[:], ALU.add))
            for t in range(NT):
                ins = nc.vector.scalar_tensor_tensor(out=x[:, t, :], in0=o_ga[1][:, t, :], scalar=lsum[:, t:t + 1],
                                                     in1=x[:, t, :], op0=ALU.subtract, op1=ALU.add)
            link(ins)
            ln_vec(3)
            hT_vec(4)
            dve.wait_ge(bn_y, 1)
            link(nc.vector.tensor_tensor(bn_y1[:], bn_y0[:], bn_y0[:], ALU.mult))
            link(nc.vector.tensor_tensor(bn_y1[:], bn_y1[:], bn_ve[:], ALU.mult))
            link(nc.vector.tensor_scalar(bn_y1[:], bn_y1[:], -0.5, 1.5, ALU.mult, ALU.add))
            link(nc.vector.tensor_tensor(bn_y1[:], bn_y1[:], bn_y0[:], ALU.mult))
            link(nc.vector.tensor_tensor(bn_s[:, 0, :], bn_y1[:], bn[:, 0, :], ALU.mult))
            link(nc.vector.tensor_tensor(bn_y1[:], bn_s[:, 0, :], bn[:, 2, :], ALU.mult))
            nc.vector.tensor_tensor(bn_s[:, 1, :], bn[:, 1, :], bn_y1[:], ALU.subtract).then_inc(bn_ok, 1)
            for t in range(NT):
                dve.wait_ge(pn_mm, t + 1)
                nc.vector.tensor_tensor(agg[:, t, :], bank[4 + t], b1, ALU.add).then_inc(pn_ok, 1)
            dve.wait_ge(bnr_mm, 2)
            for e in range(2):
                ins = nc.vector.tensor_copy(bn_rows[:, e, :], bank[(7, 0)[e]])
            ins.then_inc(bn_ok, 1)
            dve.wait_ge(ld_b3, 16)
            dve.wait_ge(ld_l3, 96)
            link(nc.vector.tensor_tensor(b_hh[:, 0:2 * F], b_hh[:, 0:2 * F], b_ih[:, 0:2 * F], ALU.add))
            for n in range(NT * 3):
                t, gate_ = divmod(n, 3)
                dve.wait_ge(gh_mm, n + 1)
                nc.vector.tensor_tensor(gh[:, t, gate_ * F:(gate_ + 1) * F], bank[GB[n]],
                                        b_hh[:, gate_ * F:(gate_ + 1) * F], ALU.add).then_inc(gh_ok, 1)
            for t in range(NT):
                ins = nc.vector.tensor_tensor(x[:, t, :], x[:, t, :], h[:, t, :], ALU.add)
            link(ins)
            for t in range(NT):
                ins = nc.vector.tensor_tensor(x[:, t, :], x[:, t, :], bn_rows[:, 1, :], ALU.add)
            link(ins)

            def lower(i, q):
                dve.wait_ge(hi_ok, i * LB + (q + 1))
                nc.vector.scalar_tensor_tensor(out=m_lo[:, q % 3, :], in0=got[:, q % LB, :], scalar=0.0,
                                               in1=m_hi[:, q % 3, :].bitcast(F32), op0=ALU.max,
                                               op1=ALU.subtract).then_inc(lo_ok, 1)

            def messages(i, first, width):
                d = dstw_f if width == WIN else dst_f
                for q in range(LB):
                    dve.wait_ge(ld_got[q], i * 16 + 16)
                    dve.wait_ge(pre_mm, i * LB + (q + 1))
                    nc.vector.tensor_tensor(got[:, q, :], got[:, q, :], bank[4 + q % 3], ALU.add).then_inc(sum_ok, 1)
                    if not (first and q < 3):
                        dve.wait_ge(scat, i * LB + (q - 2))
                    nc.vector.tensor_scalar(oh_r[:, q % 3, 0:width], iota32[:, 0:width],
                                            d[:, bass.ds(i * LB + q, 1)], None, ALU.is_equal)
                    if not (first and q < 1):
                        lower(i, q - 1)

            def all_messages(width):
                messages(0, True, width)
                with dve.Fori(1, ET // LB) as i:
                    messages(i, False, width)

            with dve.If(strays > 0):
                all_messages(N)
            with dve.Else():
                all_messages(WIN)
            lower(ET // LB - 1, LB - 1)
            dve.wait_ge(sums_ok, 2)
            for c in range(FC):
                nc.vector.tensor_copy(aggT[:, c, :], bank[c][:, PAD:PAD + N]).then_inc(aggT_ok, 1)
            for c in range(FC):
                dve.wait_ge(mT_mm, c + 1)
                nc.vector.scalar_tensor_tensor(out=mT[:, c, :], in0=deg_row[:], scalar=bn[:, 4, c:c + 1],
                                               in1=bank[4 + c][:, 0:N], op0=ALU.mult,
                                               op1=ALU.add).then_inc(mT_ok, 1)
            for t in range(NT):
                b = [(3 + 3 * t + e) % 8 for e in range(3)]
                rz, n_, d_ = grz[:, t % 2], gn[:, t % 2], gd[:, t % 2]
                dve.wait_ge(gi_mm, 3 * t + 2)
                nc.vector.tensor_tensor(rz[:, 0:F], bank[b[0]], gh[:, t, 0:F], ALU.add)
                nc.vector.tensor_tensor(rz[:, F:2 * F], bank[b[1]], gh[:, t, F:2 * F], ALU.add).then_inc(gs_v, 1)
                dve.wait_ge(gi_mm, 3 * t + 3)
                nc.vector.tensor_tensor(n_, bank[b[2]], b_ih[:, 2 * F:3 * F], ALU.add)
                dve.wait_ge(gs_s, t + 1)
                link(nc.vector.tensor_tensor(d_, rz[:, 0:F], gh[:, t, 2 * F:3 * F], ALU.mult))
                nc.vector.tensor_tensor(n_, n_, d_, ALU.add).then_inc(gn_v, 1)
                dve.wait_ge(gn_s, t + 1)
                link(nc.vector.tensor_tensor(d_, h[:, t, :], n_, ALU.subtract))
                link(nc.vector.tensor_tensor(d_, d_, rz[:, F:2 * F], ALU.mult))
                link(nc.vector.tensor_tensor(d_, d_, n_, ALU.add))
                link(nc.vector.tensor_tensor(d_, d_, bn_rows[:, 0, :], ALU.mult))
                nc.vector.tensor_tensor(x[:, t, :], x[:, t, :], d_, ALU.add).then_inc(out_ok, 1)

        @block.tensor
        def _(pe):
            def chain(o, pairs, first=True, last=True):
                for n, (l, r) in enumerate(pairs):
                    ins = nc.tensor.matmul(o, l, r, start=first and n == 0, stop=last and n == len(pairs) - 1)
                return ins

            def transpose_h():
                for c in range(FC):
                    for t in range(NT):
                        ins = nc.tensor.transpose(bank[c][:, cols(t)], h[:, t, cols(c)], ident[:])
                    ins.then_inc(hT_mm, 1)

            def attention_vectors():
                pe.wait_ge(ld_gaa, 48)
                pe.wait_ge(ld_gaT[0], 16)
                v = bank[0][:, 0:FC * 16].rearrange("p (c e n) -> p c e n", c=FC, e=2)
                for c in range(FC):
                    for hd in range(HEADS):
                        ins = nc.tensor.matmul(v[:, c, :, hd], ga_wT[0][:, hd, cols(c)], ga_a[0][:, hd, :],
                                               start=True, stop=True)
                ins.then_inc(wa_mm, 1)
                pe.wait_ge(ld_gaT[1], 16)
                v = bank[1][:, 0:2 * FC * 16].rearrange("p (c e n) -> p c e n", c=2 * FC, e=2)
                for c in range(2 * FC):
                    for j in range(FC):
                        ins = nc.tensor.matmul(v[:, c, :, 2 * j:2 * j + 2].rearrange("p s e -> p e s"),
                                               ga_wT[1][:, j, cols(c)], ga_a[1][:, :, j, :], start=True, stop=True)
                ins.then_inc(wa_mm, 1)

            def relational(l, s):
                pe.wait_ge(hT_v, 2 + FC * s)
                pe.wait_ge(ld_l1, 32)
                for t in range(NT):
                    ins = chain(bank3(4, REL)[:, t, :], [(hT[:, c, cols(t)], gw[:, l, c, :]) for c in range(FC)])
                ins.then_inc(gate_mm, 1)
                pe.wait_ge(gx_ok, REL * NT * (l + 1))
                for g in range(REL * FC):
                    r, c = divmod(g, FC)
                    cT = (c0T, c1T)[r]
                    chain(bank[YB[g]][:, 0:N], [(gx[:, r, j, cols(c)], cT[:, j, :]) for j in range(NT)]
                          ).then_inc(yT_mm, 1)
                pe.wait_ge(yT_v, REL * FC * (l + 1))
                for t in range(NT):
                    chain(bank[5 + t], [(hT[:, c, cols(t)], roots[:, l, c, :]) for c in range(FC)], last=False)
                if l == 1:
                    attention_vectors()
                for k in range(4):
                    pe.wait_ge(w_ok, 4 * l + k + 1)
                    for t in range(NT):
                        ins = chain(bank[5 + t], [(yT[:, g, cols(t)], w_mix[l][:, g * F:(g + 1) * F])
                                                  for g in (2 * k, 2 * k + 1)], first=False, last=k == 3)
                        if k == 3:
                            ins.then_inc(rg_mm, 1)

            pe.wait_ge(ident_ok, 1)
            pe.wait_ge(out_cnt, 1)
            nc.tensor.matmul(bank[7][:, 511:512], ones[:], outside[:], start=True, stop=True).then_inc(out_mm, 1)
            pe.wait_ge(h_ok, NT)
            transpose_h()
            pe.wait_ge(hT_v, 2)
            pe.wait_ge(hT_s, 2)
            pe.wait_ge(ld_l0, 64)
            chain(bank[4][0:D0, 0:N], [(wqk[:, c, 0:D0], hT[:, c, :]) for c in range(FC)]).then_inc(l0_mm, 1)
            chain(bank[5][0:D0, 0:N], [(wqk[:, c, D0:2 * D0], hT[:, c, :]) for c in range(FC)]
                  ).then_inc(l0_mm, 1)
            for t in range(NT):
                ins = chain(bank3(6, D0)[:, t, :], [(hT[:, c, cols(t)], wv[:, c, F - D0:F]) for c in range(FC)])
            ins.then_inc(l0_mm, 1)
            pe.wait_ge(hsum_ok, 1)
            chain(bank[7][:, 0:F - D0], [(hsum[:, c:c + 1].to_broadcast([P, P]), wv[:, c, 0:F - D0])
                                         for c in range(FC)]).then_inc(l0_mm, 1)

            def zeros(banks, first):
                for b in banks:
                    ins = nc.tensor.matmul(bank[b], zero[:, 0:1].to_broadcast([P, P]),
                                           zero[:, 0:1].to_broadcast([P, 512]), start=first, stop=not first)
                return ins

            def count(i, width, tiles=CB):
                for q in range(tiles):
                    k = q % EB
                    at = bass.ds(i * (CB // LB * STEP) + q // LB * STEP, WIN) if width == WIN else slice(PAD, PAD + N)
                    pe.wait_ge(oh_ok, i * CB + (q + 1))
                    for j in range(NT):
                        for e in range(2):
                            ins = nc.tensor.matmul(bank[3 * e + j][:, at], oh_s[:, k, cols(j)],
                                                   oh_d[:, k, e, 0:width], start=False, stop=False)
                    ins.then_inc(oh_used, 1)

            def all_counts(width):
                count(0, width)
                with pe.Fori(1, CT - 1) as i:
                    count(i, width)
                count(CT - 1, width, ET - CB * (CT - 1))

            pe.wait_ge(qk_ok, 2)
            zeros(range(6), True)
            pe.wait_ge(out_set, 1)
            strays = pe.value_load(outside_i[0:1, 0:1])
            with pe.If(strays > 0):
                all_counts(N)
            with pe.Else():
                all_counts(WIN)
            zeros(range(6), False).then_inc(sums_ok, 1)
            pe.wait_ge(cnt_ok, NT)
            for t in range(NT):
                nc.tensor.matmul(bank[3 + t][:, 0:N], qT[:, cols(t)], kT, start=True, stop=True).then_inc(sc_mm, 1)
            pe.wait_ge(cntn_ok, NT)
            pe.wait_ge(v_ok, 1)
            chain(bank[6][:, 0:N], [(ones[:], cnt[:, t, :]) for t in range(NT)]).then_inc(deg_mm, 1)
            pe.wait_ge(cnt_ok, NT + 1)
            for r, c_n in enumerate((c0n, c1n)):
                for t in range(NT):
                    if r == 1:
                        pe.wait_ge(cntT_ok, t + 1)
                    for j in range(NT):
                        ins = nc.tensor.transpose(bank[CB_T[r * NT + t]][:, cols(j)], c_n[:, j, cols(t)], ident[:])
                    ins.then_inc(cntn_mm, 1)
            pe.wait_ge(cntT_ok, REL * NT)
            pe.wait_ge(ex_ok, NT)
            for j in range(NT):
                for t in range(NT):
                    ins = nc.tensor.transpose(bank[j][:, cols(t)], att[:, t, cols(j)], ident[:])
                ins.then_inc(attT_mm, 1)
            pe.wait_ge(attT_ok, NT)
            for t in range(NT):
                ins = chain(bank3(7, D0)[:, t, :], [(attT[:, j, cols(t)], v7[:, j, :]) for j in range(NT)])
            ins.then_inc(o7_mm, 1)

            pe.wait_ge(h_ok, 2 * NT)
            transpose_h()
            relational(0, 1)
            pe.wait_ge(h2_ok, NT)
            transpose_h()
            relational(1, 2)

            def attention(g):
                nh, kc, inT = C[g], FC * (g + 1), (oT if g else hT)
                done = g * HEADS
                pe.wait_ge(wa_ok, g + 1)
                chain(bank[4][0:40, 0:N], [(wa[g][:, c, :], inT[:, c, :]) for c in range(kc)]).then_inc(aT_mm, 1)
                pe.wait_ge(aT_ok, 2 * g + 1)
                for t in range(NT):
                    ins = nc.tensor.transpose(bank3(5, 40)[:, t, :], aT[:, cols(t)], ident[0:40, 0:40])
                ins.then_inc(ac_mm, 1)
                pe.wait_ge(ld_ga[g], 16)
                banks, per = hx_banks(g)
                pe.wait_ge(aT_ok, 2 * g + 2)
                pe.wait_ge(aT_lo_ok, g + 1)
                steps = [(n, c) for n in range(len(banks)) for c in range(kc)]
                share = -(-len(steps) // HEADS)
                for hd in range(HEADS):
                    if hd == 1:
                        pe.wait_ge(ac_ok, g + 1)
                    if hd >= 2:
                        pe.wait_ge(far_ok, done + hd - 1)
                    chain(bank[4 + hd % 2][:, 0:N], [(pick[0:HEADS, hd:hd + 1].to_broadcast([HEADS, P]), s_)
                                                     for s_ in (aT_hi[:], aT_lo[:])]).then_inc(as_mm, 1)
                    for n, c in steps[hd * share:(hd + 1) * share]:
                        t, part = divmod(n, per)
                        ins = nc.tensor.matmul(bank[banks[n]], inT[:, c, cols(t)],
                                               ga_w[g][:, c, part * F:(part + 1) * F], start=c == 0, stop=c == kc - 1)
                        if c == kc - 1:
                            ins.then_inc(hx_mm, 1)
                pe.wait_ge(rc_ok, g + 1)
                for t in range(NT):
                    ins = nc.tensor.transpose(bank[4][0:64, cols(t)],
                                              rcols[:, t].rearrange("p e n -> p (e n)").bitcast(F32), ident[:])
                ins.then_inc(rT_mm, 1)
                pe.wait_ge(rT_ok, g + 1)
                pe.wait_ge(hx_ok, 2 * NT + g * NT)

                def row_terms(hd):
                    n = done + hd
                    if hd >= 2:
                        pe.wait_ge(lr_ok, n - 1)
                    for e in range(2):
                        both = slice(32 * e, 32 * e + 2 * HEADS)
                        nc.tensor.matmul(bank[4 + 2 * e + hd % 2][:, 0:N],
                                         pick[both, hd:hd + 1].to_broadcast([2 * HEADS, P]),
                                         rT[both, :], start=True, stop=True).then_inc(rb_mm, 1)

                row_terms(0)
                row_terms(1)
                for hd in range(HEADS):
                    n = done + hd
                    if hd + 2 < HEADS:
                        row_terms(hd + 2)
                    pe.wait_ge(pg_ok, n + 1)
                    if n >= 2:
                        pe.wait_ge(pv_used, n - 1)
                    o = bank3(hd % 2, nh + 1)
                    for j in range(NT):
                        ins = chain(o[:, j, :], [(ex[:, hd % 3, t, cols(j)], hx[g][:, t, hd, :])
                                                 for t in range(NT)])
                    ins.then_inc(pv_mm, 1)

            pe.wait_ge(h_ok, 3 * NT)
            transpose_h()
            pe.wait_ge(hT_v, 2 * 2 + FC * 2)
            pe.wait_ge(hT_s, 2 * 2)
            attention(0)
            pe.wait_ge(pv_used, HEADS)
            for c in range(2 * FC):
                for t in range(NT):
                    ins = nc.tensor.transpose(bank[c][:, cols(t)], o_ga[0][:, t, cols(c)], ident[:])
                ins.then_inc(oT_mm, 1)
            pe.wait_ge(oT_v, FC)
            pe.wait_ge(oT_s, FC)
            pe.wait_ge(set_ok, 2)
            attention(1)

            pe.wait_ge(h_ok, 4 * NT)
            transpose_h()
            pe.wait_ge(hT_v, 2 * 3 + FC * 2)
            pe.wait_ge(hT_s, 2 * 3)
            pe.wait_ge(ld_l3, 96)
            for t in range(NT):
                chain(bank[4 + t], [(hT[:, c, cols(t)], w1a[:, c, :]) for c in range(FC)]).then_inc(pn_mm, 1)
            pe.wait_ge(bn_ok, 1)
            for e in range(2):
                for c in range(FC):
                    ins = nc.tensor.matmul(bank[(7, 0)[e]][:, cols(c)], bn_s[:, e, c:c + 1].to_broadcast([P, P]),
                                           ident[:], start=True, stop=True)
                ins.then_inc(bnr_mm, 1)
            for n in range(NT * 3):
                t, gate_ = divmod(n, 3)
                if n >= 3:
                    pe.wait_ge(gh_ok, n - 2)
                chain(bank[GB[n]], [(hT[:, c, cols(t)], w_hh[:, c, gate_ * F:(gate_ + 1) * F])
                                    for c in range(FC)]).then_inc(gh_mm, 1)
            pe.wait_ge(gh_ok, 9)
            pe.wait_ge(bn_ok, 2)

            def edge_part(i, q, first):
                if q % LC == 0:
                    pe.wait_ge(ld_ea[q // LC], i * 32 + 32)
                if not (first and q < 3):
                    pe.wait_ge(sum_ok, i * LB + (q - 2))
                nc.tensor.matmul(bank[4 + q % 3], ea[:, q // LC, cols(q % LC)], w1b[:], start=True, stop=True
                                 ).then_inc(pre_mm, 1)

            def scatter_all(i, q):
                pe.wait_ge(lo_ok, i * LB + (q + 1))
                for c in range(FC):
                    for m in (m_hi, m_lo):
                        ins = nc.tensor.matmul(bank[c][:, PAD:PAD + N], m[:, q % 3, cols(c)], oh_r[:, q % 3, :],
                                               start=False, stop=False)
                ins.then_inc(scat, 1)

            def scatter(i, q):
                if q == 0 and not (isinstance(i, int) and i == 0):
                    pe.wait_ge(z_ok, i)
                pe.wait_ge(lo_ok, i * LB + (q + 1))
                for m in (m_hi, m_lo):
                    ins = nc.tensor.matmul(bank[7][0:WIN, :], oh_r[:, q % 3, 0:WIN], m[:, q % 3, :],
                                           start=m is m_hi and q == 0, stop=m is m_lo and q % LB == LB - 1)
                ins.then_inc(scat, 1)

            def sums_all():
                for q in range(LB):
                    edge_part(0, q, True)
                    if q >= LAG:
                        scatter_all(0, q - LAG)
                with pe.Fori(1, ET // LB) as i:
                    for q in range(LB):
                        edge_part(i, q, False)
                        scatter_all(i, q - LAG)
                for q in range(LB - LAG, LB):
                    scatter_all(ET // LB - 1, q)

            def sums_windows():
                def add_window(i):
                    pe.wait_ge(z_ok, i + 1)
                    for c in range(FC):
                        ins = nc.tensor.matmul(bank[c][:, bass.ds(i * STEP, WIN)], zs[:, cols(c)],
                                               ident[0:WIN, 0:WIN], start=False, stop=False)
                    ins.then_inc(z_used, 1)

                def turn(i, first):
                    for q in range(LB):
                        edge_part(i, q, first)
                        if not (first and q < LAG):
                            scatter(i, q - LAG)
                        if q == 4 and not first:
                            add_window(i - 1)

                turn(0, True)
                with pe.Fori(1, ET // LB) as i:
                    turn(i, False)
                for q in range(LB - LAG, LB):
                    scatter(ET // LB - 1, q)
                add_window(ET // LB - 1)

            zeros(range(FC), True)
            with pe.If(strays > 0):
                sums_all()
            with pe.Else():
                sums_windows()
            zeros(range(FC), False).then_inc(sums_ok, 1)
            pe.wait_ge(aggT_ok, FC)
            pe.wait_ge(ld_ih, 32)
            for c in range(FC):
                chain(bank[4 + c][:, 0:N], [(w2[:, k, cols(c)], aggT[:, k, :]) for k in range(FC)]
                      ).then_inc(mT_mm, 1)
            pe.wait_ge(mT_ok, FC)
            for t in range(NT):
                for e in range(3):
                    if t == 2 and e == 2:
                        pe.wait_ge(gs_v, 1)
                    chain(bank[(3 + 3 * t + e) % 8], [(mT[:, c, cols(t)], w_ih[:, c, e * F:(e + 1) * F])
                                                      for c in range(FC)]).then_inc(gi_mm, 1)


def kernel(**inputs):
    import numpy as np
    import concourse.bacc as bacc
    from concourse.bass_utils import run_bass_kernel_spmd

    def get(name):
        return np.asarray(inputs[name])

    def chunks(w):
        return w.reshape(-1, P, w.shape[1]).transpose(1, 0, 2)

    def halves(basis):
        return basis.reshape(-1, 2, 2, P, F).transpose(3, 0, 1, 2, 4).reshape(P, -1, HALF)

    basis = [get("L1_gnn_basis1"), get("L1_gnn_basis2")]
    lay = {
        "x": chunks(get("x")),
        "edge": np.stack([get(n).reshape(ET, P).T for n in ("src", "dst", "edge_type_2")], axis=1),
        "wqk": chunks(np.concatenate([get("L0_gnn_Wq")[:, F - D0:], get("L0_gnn_Wk")[:, F - D0:]], axis=1)),
        "bqk": np.stack([get("L0_gnn_bq")[F - D0:], get("L0_gnn_bk")[F - D0:]], axis=1),
        "wv": chunks(get("L0_gnn_Wv")),
        "rows": np.stack([get("L0_gnn_bv"), get("L1_gnn_bias1"), get("L1_gnn_bias2")]),
        "mixc": np.stack([get("L1_gnn_att1").T, get("L1_gnn_att2").T]),
        "gw": np.stack([get(f"L1_gnn_gate_w{l}")[:, :, 0].reshape(REL, FC, P).transpose(2, 1, 0) for l in (1, 2)], axis=1),
        "roots": np.stack([chunks(get("L1_gnn_root1")), chunks(get("L1_gnn_root2"))], axis=1),
        "basis_v": np.concatenate([halves(b[:MIX_V]) for b in basis], axis=1),
        "basis_g": np.concatenate([halves(b[MIX_V:]) for b in basis], axis=1),
        "ga_w1": chunks(get("L2_gnn_W1")),
        "ga_w1T": chunks(get("L2_gnn_W1").T),
        "ga_w2": chunks(get("L2_gnn_W2")),
        "ga_w2T": chunks(get("L2_gnn_W2").T),
        "ga_a1": np.stack([get("L2_gnn_att_src1"), get("L2_gnn_att_dst1")]).transpose(2, 1, 0),
        "ga_a2": np.stack([get("L2_gnn_att_src2"), get("L2_gnn_att_dst2")]).reshape(2, FC, 2, C2).transpose(3, 2, 1, 0),
        "ga_b": np.concatenate([get("L2_gnn_b1"), get("L2_gnn_b2")]),
        "edge_attr": get("edge_attr_128").T.reshape(ED, ET // LC, LC * P),
        "src_idx": get("src").reshape(ET // LC, LC, P).transpose(2, 0, 1),
        "w1a": chunks(get("L3_gnn_W1").T[:F]),
        "w1b": get("L3_gnn_W1").T[F:],
        "b1": get("L3_gnn_b1"),
        "w2": chunks(get("L3_gnn_W2").T),
        "w_ih": chunks(get("L3_gnn_W_ih").T),
        "w_hh": chunks(get("L3_gnn_W_hh").T),
        "b_ih": get("L3_gnn_b_ih"),
        "b_hh": get("L3_gnn_b_hh"),
        "bn": np.stack([get(f"L3_gnn_{n}").reshape(FC, P).T for n in ("gamma", "beta", "run_mean", "run_var", "b2")], axis=1),
    }
    nc = bacc.Bacc("TRN2", target_bir_lowering=False, num_devices=1)
    arrays, aps = {}, {}
    for name, v in lay.items():
        v = np.ascontiguousarray(v)
        arrays[f"{name}_dram"] = v
        aps[name] = nc.dram_tensor(f"{name}_dram", v.shape, mybir.dt.from_np(v.dtype), kind="ExternalInput").ap()
    out = nc.dram_tensor("out_dram", (N, F), F32, kind="ExternalOutput").ap()
    build(nc, aps, out.rearrange("(t p) n -> p t n", p=P))
    r = run_bass_kernel_spmd(nc, [arrays], core_ids=[0])
    return r.results[0]["out_dram"]
```
